# Optimizing a Trainium2 kernel written in Bass

```python
import numpy as np
import jax
import jax.numpy as jnp

def _softmax(x, axis=-1):
    return jax.nn.softmax(x, axis=axis)

def _gelu(x):
    return jax.nn.gelu(x, approximate=True)

def _silu(x):
    return jax.nn.silu(x)

def _sigmoid(x):
    return jax.nn.sigmoid(x)

def _layernorm(x, axis=-1, eps=1e-05):
    m = jnp.mean(x, axis=axis, keepdims=True)
    v = jnp.var(x, axis=axis, keepdims=True)
    return (x - m) / jnp.sqrt(v + eps)

def _scatter_add(tgt, idx, src, axis=0):
    return tgt.at[idx].add(src)

def _segment_sum(src, seg, n):
    return jax.ops.segment_sum(src, seg, n)
kernel_name = 'mk_perceiver_d2_seqx_r8_5f9300'

def setup_inputs(seed: int=0):
    np.random.seed(seed)
    _w = jnp.asarray

    def _rec_inputs():
        import jax
        import jax.numpy as jnp
        _rk = jax.random.key(seed)
        x = -0.0003929 + 0.9999 * jax.random.normal(jax.random.fold_in(_rk, 1), (2, 128, 256), jnp.float32)
        _lenS = 128 - jax.random.randint(jax.random.fold_in(_rk, 7), (2,), 0, max(1, 128 // 4) + 1, jnp.int32)
        _lenS2 = 2048 - jax.random.randint(jax.random.fold_in(_rk, 8), (2,), 0, max(1, 2048 // 4) + 1, jnp.int32)
        _ctx_2048P = jax.random.normal(jax.random.fold_in(_rk, 11), (2, 16, 256), jnp.float32)
        _ctx_2048c = jax.random.dirichlet(jax.random.fold_in(_rk, 511), 0.3 * jnp.ones((16,), jnp.float32), (2, 2048))
        _ctx_2048t = jnp.einsum('bsk,bkd->bsd', _ctx_2048c, _ctx_2048P)
        _ctx_2048t = _ctx_2048t * jax.lax.rsqrt(jnp.mean(jnp.square(_ctx_2048t)) + 1e-12) * 0.953939
        ctx_2048 = -0.000514642 + 1.00011 * (_ctx_2048t + 0.3 * jax.random.normal(jax.random.fold_in(_rk, 611), (2, 2048, 256), jnp.float32))
        return (x, ctx_2048)
    x, ctx_2048 = _rec_inputs()

    def _L0_xattn_setup():
        import jax, jax.numpy as jnp
        import numpy as np
        DIM = 256
        NHEADS = 32
        HEAD_DIM = DIM // NHEADS
        EPS = 1e-06

        def _rmsnorm(t):
            return t * jax.lax.rsqrt(jnp.mean(t * t, axis=-1, keepdims=True) + EPS)
        key = jax.random.key(seed)
        kx, kc, kq, kk, kv = jax.random.split(key, 5)
        x = jax.random.normal(kx, (2, 512, DIM), dtype=jnp.float32)
        context = jax.random.normal(kc, (2, 64, DIM), dtype=jnp.float32)
        std = 0.02
        Wq = jax.random.normal(kq, (DIM, DIM), dtype=jnp.float32) * std
        Wk = jax.random.normal(kk, (DIM, DIM), dtype=jnp.float32) * std
        Wv = jax.random.normal(kv, (DIM, DIM), dtype=jnp.float32) * std
        return {'x': x, 'context': context, 'Wq': Wq, 'Wk': Wk, 'Wv': Wv}
    _L0_xattn_all = _L0_xattn_setup()
    _L0_xattn_in = {k: v for k, v in _L0_xattn_all.items() if k in ('Wq', 'Wk', 'Wv')}
    del _L0_xattn_all

    def _L0_attn_setup():
        import jax, jax.numpy as jnp
        import numpy as np
        B, T, D_MODEL = (4, 256, 256)
        NUM_HEADS, HEAD_SIZE = (16, 128)
        MODEL_SIZE = 256
        key = jax.random.key(seed)
        ks = jax.random.split(key, 9)
        s = 0.02 / np.sqrt(D_MODEL)
        so = 0.02 / np.sqrt(NUM_HEADS * HEAD_SIZE)
        return {'query': jax.random.normal(ks[0], (B, T, D_MODEL), jnp.float32), 'w_q': jax.random.normal(ks[1], (D_MODEL, NUM_HEADS * HEAD_SIZE), jnp.float32) * s, 'b_q': jnp.zeros((NUM_HEADS * HEAD_SIZE,), jnp.float32), 'w_k': jax.random.normal(ks[2], (D_MODEL, NUM_HEADS * HEAD_SIZE), jnp.float32) * s, 'b_k': jnp.zeros((NUM_HEADS * HEAD_SIZE,), jnp.float32), 'w_v': jax.random.normal(ks[3], (D_MODEL, NUM_HEADS * HEAD_SIZE), jnp.float32) * s, 'b_v': jnp.zeros((NUM_HEADS * HEAD_SIZE,), jnp.float32), 'w_o': jax.random.normal(ks[4], (NUM_HEADS * HEAD_SIZE, MODEL_SIZE), jnp.float32) * so, 'b_o': jnp.zeros((MODEL_SIZE,), jnp.float32)}
    _L0_attn_all = _L0_attn_setup()
    _L0_attn_in = {k: v for k, v in _L0_attn_all.items() if k in ('w_q', 'b_q', 'w_k', 'b_k', 'w_v', 'b_v', 'w_o', 'b_o')}
    del _L0_attn_all

    def _L0_ffn_setup():
        import jax, jax.numpy as jnp
        import numpy as np
        D_MODEL = 256
        HIDDEN = int(2 * D_MODEL * 4 / 3)

        def ternary_quant(w):
            s = jnp.mean(jnp.abs(w))
            q = jnp.clip(jnp.round(w / s), -1.0, 1.0) * s
            return w + jax.lax.stop_gradient(q - w)
        key = jax.random.key(seed)
        k0, k1, k2, k3 = jax.random.split(key, 4)
        x = jax.random.normal(k0, (4, 512, D_MODEL), dtype=jnp.float32)
        std_in = 1.0 / np.sqrt(D_MODEL)
        std_h = 1.0 / np.sqrt(HIDDEN)
        w1 = jax.random.uniform(k1, (HIDDEN, D_MODEL), jnp.float32, -std_in, std_in)
        w3 = jax.random.uniform(k2, (HIDDEN, D_MODEL), jnp.float32, -std_in, std_in)
        w2 = jax.random.uniform(k3, (D_MODEL, HIDDEN), jnp.float32, -std_h, std_h)
        return {'x': x, 'w1': w1, 'w3': w3, 'w2': w2}
    _L0_ffn_all = _L0_ffn_setup()
    _L0_ffn_in = {k: v for k, v in _L0_ffn_all.items() if k in ('w1', 'w3', 'w2')}
    del _L0_ffn_all

    def _L1_xattn_setup():
        import jax, jax.numpy as jnp
        import numpy as np
        from jax import lax
        LN_EPS = 1e-05
        key = jax.random.key(seed)
        ks = jax.random.split(key, 8)
        B, S, T, D = (4, 128, 256, 256)
        scale = 0.02
        return {'Z': jax.random.normal(ks[0], (B, S, D), dtype=jnp.float32), 'kv': jax.random.normal(ks[1], (B, T, D), dtype=jnp.float32), 'decay': jnp.float32(0.9), 'W_in': jax.random.normal(ks[2], (D, D), dtype=jnp.float32) * scale, 'b_in': jnp.zeros((D,), dtype=jnp.float32), 'W_out': jax.random.normal(ks[3], (D, D), dtype=jnp.float32) * scale, 'b_out': jnp.zeros((D,), dtype=jnp.float32), 'gamma': jnp.ones((D,), dtype=jnp.float32), 'beta': jnp.zeros((D,), dtype=jnp.float32)}
    _L1_xattn_all = _L1_xattn_setup()
    _L1_xattn_in = {k: v for k, v in _L1_xattn_all.items() if k in ('decay', 'W_in', 'b_in', 'W_out', 'b_out', 'gamma', 'beta')}
    del _L1_xattn_all

    def _L1_attn_setup():
        import jax, jax.numpy as jnp
        import numpy as np
        from jax import lax
        B, L, D = (2, 512, 256)
        K, KQ, M, H = (32, 4, 8, 8)
        MEM = K * H
        FLAT = K * H * M
        CONV_W = 4
        DIM_SWIGLU = H * 3 * 2
        N_DECAY = K - 4

        def _forward(x, W_mem, conv_k, W_q, theta, decay_slopes, anchor_slopes, score_scale, W_re, W_im, norm_scale, W_out):
            b, l, d = x.shape
            z = x @ W_mem
            z = lax.conv_general_dilated(z, conv_k, window_strides=(1,), padding=[(CONV_W - 1, 0)], dimension_numbers=('NHC', 'HIO', 'NHC'), feature_group_count=MEM + K)
            k_val = z[..., :MEM].reshape(b, l, K, H)
            s_raw = z[..., MEM:].reshape(b, l, K, 1)
            q = (x @ W_q).reshape(b, l, KQ, H, M, 2)
            q_re, q_im = (q[..., 0], q[..., 1])
            pos = jnp.arange(l, dtype=jnp.float32)
            slopes_d = jax.nn.softplus(decay_slopes).reshape(1, 1, -1, 1)
            slopes_a = jax.nn.softplus(anchor_slopes).reshape(1, 1, -1, 1)
            dist = jnp.maximum(jnp.float32(l - 1) - pos, 0.0)
            log_w = jnp.concatenate([-slopes_d * dist[None, :, None, None], -slopes_a * pos[None, :, None, None]], axis=2)
            log_p = jnp.clip(score_scale[None, None, :, None] * s_raw, -20.0, 20.0)
            p_w = jnp.exp(log_p + log_w)
            phi = k_val[..., None] * theta
            re_k, im_k = (jnp.cos(phi), jnp.sin(phi))
            pw5 = p_w[..., None]
            merged = jnp.concatenate([p_w.squeeze(-1), (pw5 * re_k).reshape(b, l, FLAT), (pw5 * im_k).reshape(b, l, FLAT)], axis=-1)
            cs = jnp.cumsum(merged, axis=1)
            den = cs[..., :K]
            num_re = cs[..., K:K + FLAT]
            num_im = cs[..., K + FLAT:]
            inv_den = 1.0 / jnp.maximum(den[..., None], 0.0001)
            state_re = num_re.reshape(b, l, K, H, M) * inv_den[..., None]
            state_im = num_im.reshape(b, l, K, H, M) * inv_den[..., None]
            n_rep = K // KQ
            q_re = jnp.repeat(q_re, n_rep, axis=2)
            q_im = jnp.repeat(q_im, n_rep, axis=2)
            out_re = jnp.sum(state_re * q_re + state_im * q_im, axis=-1)
            out_im = jnp.sum(state_im * q_re - state_re * q_im, axis=-1)
            out_re = out_re * norm_scale
            out_im = out_im * norm_scale
            y = jnp.einsum('blkh,khn->blkn', out_re, W_re) + jnp.einsum('blkh,khn->blkn', out_im, W_im)
            y_val, y_gate = jnp.split(y, 2, axis=-1)
            y = (y_val * jax.nn.silu(y_gate)).reshape(b, l, -1)
            return y @ W_out
        key = jax.random.key(seed)
        ks = jax.random.split(key, 8)
        x = jax.random.normal(ks[0], (B, L, D), dtype=jnp.float32)
        W_mem = jax.random.normal(ks[1], (D, MEM + K), dtype=jnp.float32) / np.sqrt(D)
        conv_k = jax.random.normal(ks[2], (CONV_W, 1, MEM + K), dtype=jnp.float32) * 0.3
        W_q = jax.random.normal(ks[3], (D, KQ * H * M * 2), dtype=jnp.float32) / np.sqrt(D)
        theta = jnp.asarray(np.tile(np.geomspace(0.001, 3.0, M).reshape(1, 1, 1, 1, M), (1, 1, K, H, 1)), dtype=jnp.float32)
        decay_slopes = jnp.asarray(np.log(np.expm1(np.geomspace(0.001, 0.1, N_DECAY))), dtype=jnp.float32)
        anchor_slopes = jnp.asarray(np.log(np.expm1(np.geomspace(0.01, 0.1, 4))), dtype=jnp.float32)
        score_scale = jnp.ones((K,), dtype=jnp.float32)
        g = np.sqrt(2.0 / (H + DIM_SWIGLU))
        W_re = jax.random.normal(ks[4], (K, H, DIM_SWIGLU), dtype=jnp.float32) * g
        W_im = jax.random.normal(ks[5], (K, H, DIM_SWIGLU), dtype=jnp.float32) * g
        norm_scale = jnp.ones((1, 1, K, H), dtype=jnp.float32)
        W_out = jax.random.normal(ks[6], (K * H * 3, D), dtype=jnp.float32) / np.sqrt(K * H * 3)
        return {'x': x, 'W_mem': W_mem, 'conv_k': conv_k, 'W_q': W_q, 'theta': theta, 'decay_slopes': decay_slopes, 'anchor_slopes': anchor_slopes, 'score_scale': score_scale, 'W_re': W_re, 'W_im': W_im, 'norm_scale': norm_scale, 'W_out': W_out}
    _L1_attn_all = _L1_attn_setup()
    _L1_attn_in = {k: v for k, v in _L1_attn_all.items() if k in ('W_mem', 'conv_k', 'W_q', 'theta', 'decay_slopes', 'anchor_slopes', 'score_scale', 'W_re', 'W_im', 'norm_scale', 'W_out')}
    del _L1_attn_all

    def _L1_ffn_setup():
        import jax, jax.numpy as jnp
        import numpy as np
        B, S, H = (4, 128, 256)
        E, K, I, SI = (16, 4, 176, 704)

        def _silu_mul(gu, inter):
            return jax.nn.silu(gu[:, :inter]) * gu[:, inter:]
        key = jax.random.key(seed)
        ks = jax.random.split(key, 7)
        s = 0.02
        return {'hidden_states': jax.random.normal(ks[0], (B, S, H), jnp.float32), 'gate_w': jax.random.normal(ks[1], (E, H), jnp.float32) * s, 'expert_gate_up': jax.random.normal(ks[2], (E, 2 * I, H), jnp.float32) * s, 'expert_down': jax.random.normal(ks[3], (E, H, I), jnp.float32) * s, 'shared_gate_up': jax.random.normal(ks[4], (2 * SI, H), jnp.float32) * s, 'shared_down': jax.random.normal(ks[5], (H, SI), jnp.float32) * s, 'shared_gate_vec': jax.random.normal(ks[6], (1, H), jnp.float32) * s}
    _L1_ffn_all = _L1_ffn_setup()
    _L1_ffn_in = {k: v for k, v in _L1_ffn_all.items() if k in ('gate_w', 'expert_gate_up', 'expert_down', 'shared_gate_up', 'shared_down', 'shared_gate_vec')}
    del _L1_ffn_all
    return {'x': x, 'ctx_2048': ctx_2048, 'L0_xattn_Wq': _L0_xattn_in['Wq'], 'L0_xattn_Wk': _L0_xattn_in['Wk'], 'L0_xattn_Wv': _L0_xattn_in['Wv'], 'L0_attn_w_q': _L0_attn_in['w_q'], 'L0_attn_b_q': _L0_attn_in['b_q'], 'L0_attn_w_k': _L0_attn_in['w_k'], 'L0_attn_b_k': _L0_attn_in['b_k'], 'L0_attn_w_v': _L0_attn_in['w_v'], 'L0_attn_b_v': _L0_attn_in['b_v'], 'L0_attn_w_o': _L0_attn_in['w_o'], 'L0_attn_b_o': _L0_attn_in['b_o'], 'L0_ffn_w1': _L0_ffn_in['w1'], 'L0_ffn_w3': _L0_ffn_in['w3'], 'L0_ffn_w2': _L0_ffn_in['w2'], 'L1_xattn_decay': _L1_xattn_in['decay'], 'L1_xattn_W_in': _L1_xattn_in['W_in'], 'L1_xattn_b_in': _L1_xattn_in['b_in'], 'L1_xattn_W_out': _L1_xattn_in['W_out'], 'L1_xattn_b_out': _L1_xattn_in['b_out'], 'L1_xattn_gamma': _L1_xattn_in['gamma'], 'L1_xattn_beta': _L1_xattn_in['beta'], 'L1_attn_W_mem': _L1_attn_in['W_mem'], 'L1_attn_conv_k': _L1_attn_in['conv_k'], 'L1_attn_W_q': _L1_attn_in['W_q'], 'L1_attn_theta': _L1_attn_in['theta'], 'L1_attn_decay_slopes': _L1_attn_in['decay_slopes'], 'L1_attn_anchor_slopes': _L1_attn_in['anchor_slopes'], 'L1_attn_score_scale': _L1_attn_in['score_scale'], 'L1_attn_W_re': _L1_attn_in['W_re'], 'L1_attn_W_im': _L1_attn_in['W_im'], 'L1_attn_norm_scale': _L1_attn_in['norm_scale'], 'L1_attn_W_out': _L1_attn_in['W_out'], 'L1_ffn_gate_w': _L1_ffn_in['gate_w'], 'L1_ffn_expert_gate_up': _L1_ffn_in['expert_gate_up'], 'L1_ffn_expert_down': _L1_ffn_in['expert_down'], 'L1_ffn_shared_gate_up': _L1_ffn_in['shared_gate_up'], 'L1_ffn_shared_down': _L1_ffn_in['shared_down'], 'L1_ffn_shared_gate_vec': _L1_ffn_in['shared_gate_vec']}

def reference(x, ctx_2048, L0_xattn_Wq, L0_xattn_Wk, L0_xattn_Wv, L0_attn_w_q, L0_attn_b_q, L0_attn_w_k, L0_attn_b_k, L0_attn_w_v, L0_attn_b_v, L0_attn_w_o, L0_attn_b_o, L0_ffn_w1, L0_ffn_w3, L0_ffn_w2, L1_xattn_decay, L1_xattn_W_in, L1_xattn_b_in, L1_xattn_W_out, L1_xattn_b_out, L1_xattn_gamma, L1_xattn_beta, L1_attn_W_mem, L1_attn_conv_k, L1_attn_W_q, L1_attn_theta, L1_attn_decay_slopes, L1_attn_anchor_slopes, L1_attn_score_scale, L1_attn_W_re, L1_attn_W_im, L1_attn_norm_scale, L1_attn_W_out, L1_ffn_gate_w, L1_ffn_expert_gate_up, L1_ffn_expert_down, L1_ffn_shared_gate_up, L1_ffn_shared_down, L1_ffn_shared_gate_vec):
    import jax
    import jax.numpy as jnp

    def _L0_xattn_ref(x, context, Wq, Wk, Wv):
        import jax, jax.numpy as jnp
        import numpy as np
        DIM = 256
        NHEADS = 32
        HEAD_DIM = DIM // NHEADS
        EPS = 1e-06

        def _rmsnorm(t):
            return t * jax.lax.rsqrt(jnp.mean(t * t, axis=-1, keepdims=True) + EPS)
        b, n, _ = x.shape
        m = context.shape[1]
        q = x @ Wq.T
        k_raw = context @ Wk.T
        v_raw = context @ Wv.T
        q = q.reshape(b, n, NHEADS, HEAD_DIM).transpose(0, 2, 1, 3)
        kv = jnp.concatenate([k_raw, v_raw], axis=-1)
        kv = kv.reshape(b, m, NHEADS, HEAD_DIM, 2)
        k = kv[..., 0].transpose(0, 2, 1, 3)
        v = kv[..., 1].transpose(0, 2, 1, 3)
        q = _rmsnorm(q)
        k = _rmsnorm(k)
        scale = HEAD_DIM ** (-0.5)
        scores = jnp.einsum('bhnd,bhmd->bhnm', q, k) * scale
        attn = jax.nn.softmax(scores, axis=-1)
        out = jnp.einsum('bhnm,bhmd->bhnd', attn, v)
        return out.transpose(0, 2, 1, 3).reshape(b, n, NHEADS * HEAD_DIM)

    def _L0_attn_ref(query, w_q, b_q, w_k, b_k, w_v, b_v, w_o, b_o):
        import jax, jax.numpy as jnp
        import numpy as np
        B, T, D_MODEL = (4, 256, 256)
        NUM_HEADS, HEAD_SIZE = (16, 128)
        MODEL_SIZE = 256
        B_, T_, _ = query.shape
        q = (query @ w_q + b_q).reshape(B_, T_, NUM_HEADS, HEAD_SIZE)
        k = (query @ w_k + b_k).reshape(B_, T_, NUM_HEADS, HEAD_SIZE)
        v = (query @ w_v + b_v).reshape(B_, T_, NUM_HEADS, HEAD_SIZE)
        logits = jnp.einsum('bthd,bThd->bhtT', q, k) * jax.lax.rsqrt(jnp.float32(HEAD_SIZE))
        i = jnp.arange(T_, dtype=jnp.int32)[:, None]
        j = jnp.arange(T_, dtype=jnp.int32)
        mask = (i >= j).astype(logits.dtype)
        logits = logits - 10000000000.0 * (1.0 - mask)
        weights = jax.nn.softmax(logits, axis=-1)
        attn = jnp.einsum('bhtT,bThd->bthd', weights, v).reshape(B_, T_, NUM_HEADS * HEAD_SIZE)
        out = attn @ w_o + b_o
        return out

    def _L0_ffn_ref(x, w1, w3, w2):
        import jax, jax.numpy as jnp
        import numpy as np
        D_MODEL = 256
        HIDDEN = int(2 * D_MODEL * 4 / 3)

        def ternary_quant(w):
            s = jnp.mean(jnp.abs(w))
            q = jnp.clip(jnp.round(w / s), -1.0, 1.0) * s
            return w + jax.lax.stop_gradient(q - w)
        w1q = ternary_quant(w1)
        w3q = ternary_quant(w3)
        w2q = ternary_quant(w2)
        h1 = jnp.einsum('bsd,hd->bsh', x, w1q)
        h3 = jnp.einsum('bsd,hd->bsh', x, w3q)
        g = jax.nn.silu(h1) * h3
        return jnp.einsum('bsh,dh->bsd', g, w2q)

    def _L1_xattn_ref(Z, kv, decay, W_in, b_in, W_out, b_out, gamma, beta):
        import jax, jax.numpy as jnp
        import numpy as np
        from jax import lax
        LN_EPS = 1e-05
        B, T, D = kv.shape
        K = jax.nn.sigmoid(decay)
        x = jnp.einsum('btd,ed->bte', kv, W_in) + b_in

        def scan_fn(s, xt):
            s = K * s + xt
            return (s, s)
        s0 = jnp.zeros((B, D), dtype=kv.dtype)
        _, states = lax.scan(scan_fn, s0, jnp.swapaxes(x, 0, 1))
        states = jnp.swapaxes(states, 0, 1)
        proj = jnp.einsum('btd,ed->bte', states, W_out) + b_out
        summary = jnp.mean(proj, axis=1, keepdims=True)
        y = Z + summary
        mu = jnp.mean(y, axis=-1, keepdims=True)
        var = jnp.mean((y - mu) ** 2, axis=-1, keepdims=True)
        return (y - mu) / jnp.sqrt(var + LN_EPS) * gamma + beta

    def _L1_attn_ref(x, W_mem, conv_k, W_q, theta, decay_slopes, anchor_slopes, score_scale, W_re, W_im, norm_scale, W_out):
        import jax, jax.numpy as jnp
        import numpy as np
        from jax import lax
        B, L, D = (2, 512, 256)
        K, KQ, M, H = (32, 4, 8, 8)
        MEM = K * H
        FLAT = K * H * M
        CONV_W = 4
        DIM_SWIGLU = H * 3 * 2
        N_DECAY = K - 4

        def _forward(x, W_mem, conv_k, W_q, theta, decay_slopes, anchor_slopes, score_scale, W_re, W_im, norm_scale, W_out):
            b, l, d = x.shape
            z = x @ W_mem
            z = lax.conv_general_dilated(z, conv_k, window_strides=(1,), padding=[(CONV_W - 1, 0)], dimension_numbers=('NHC', 'HIO', 'NHC'), feature_group_count=MEM + K)
            k_val = z[..., :MEM].reshape(b, l, K, H)
            s_raw = z[..., MEM:].reshape(b, l, K, 1)
            q = (x @ W_q).reshape(b, l, KQ, H, M, 2)
            q_re, q_im = (q[..., 0], q[..., 1])
            pos = jnp.arange(l, dtype=jnp.float32)
            slopes_d = jax.nn.softplus(decay_slopes).reshape(1, 1, -1, 1)
            slopes_a = jax.nn.softplus(anchor_slopes).reshape(1, 1, -1, 1)
            dist = jnp.maximum(jnp.float32(l - 1) - pos, 0.0)
            log_w = jnp.concatenate([-slopes_d * dist[None, :, None, None], -slopes_a * pos[None, :, None, None]], axis=2)
            log_p = jnp.clip(score_scale[None, None, :, None] * s_raw, -20.0, 20.0)
            p_w = jnp.exp(log_p + log_w)
            phi = k_val[..., None] * theta
            re_k, im_k = (jnp.cos(phi), jnp.sin(phi))
            pw5 = p_w[..., None]
            merged = jnp.concatenate([p_w.squeeze(-1), (pw5 * re_k).reshape(b, l, FLAT), (pw5 * im_k).reshape(b, l, FLAT)], axis=-1)
            cs = jnp.cumsum(merged, axis=1)
            den = cs[..., :K]
            num_re = cs[..., K:K + FLAT]
            num_im = cs[..., K + FLAT:]
            inv_den = 1.0 / jnp.maximum(den[..., None], 0.0001)
            state_re = num_re.reshape(b, l, K, H, M) * inv_den[..., None]
            state_im = num_im.reshape(b, l, K, H, M) * inv_den[..., None]
            n_rep = K // KQ
            q_re = jnp.repeat(q_re, n_rep, axis=2)
            q_im = jnp.repeat(q_im, n_rep, axis=2)
            out_re = jnp.sum(state_re * q_re + state_im * q_im, axis=-1)
            out_im = jnp.sum(state_im * q_re - state_re * q_im, axis=-1)
            out_re = out_re * norm_scale
            out_im = out_im * norm_scale
            y = jnp.einsum('blkh,khn->blkn', out_re, W_re) + jnp.einsum('blkh,khn->blkn', out_im, W_im)
            y_val, y_gate = jnp.split(y, 2, axis=-1)
            y = (y_val * jax.nn.silu(y_gate)).reshape(b, l, -1)
            return y @ W_out
        return _forward(x, W_mem, conv_k, W_q, theta, decay_slopes, anchor_slopes, score_scale, W_re, W_im, norm_scale, W_out)

    def _L1_ffn_ref(hidden_states, gate_w, expert_gate_up, expert_down, shared_gate_up, shared_down, shared_gate_vec):
        import jax, jax.numpy as jnp
        import numpy as np
        B, S, H = (4, 128, 256)
        E, K, I, SI = (16, 4, 176, 704)

        def _silu_mul(gu, inter):
            return jax.nn.silu(gu[:, :inter]) * gu[:, inter:]
        orig_shape = hidden_states.shape
        x = hidden_states.reshape(-1, H)
        router_logits = x @ gate_w.T
        routing_probs = jax.nn.softmax(router_logits.astype(jnp.float32), axis=-1)
        topk_w, topk_idx = jax.lax.top_k(routing_probs, K)
        topk_w = topk_w / topk_w.sum(axis=-1, keepdims=True)
        topk_w = topk_w.astype(x.dtype)
        combine = (jax.nn.one_hot(topk_idx, E, dtype=x.dtype) * topk_w[..., None]).sum(1)
        shared = _silu_mul(x @ shared_gate_up.T, SI) @ shared_down.T
        shared = shared * jax.nn.sigmoid(x @ shared_gate_vec.T)

        def step(acc, ew):
            w_gu, w_d, cw = ew
            h = _silu_mul(x @ w_gu.T, I)
            return (acc + h @ w_d.T * cw[:, None], None)
        acc0 = jnp.zeros_like(x)
        sparse, _ = jax.lax.scan(step, acc0, (expert_gate_up, expert_down, combine.T))
        return (shared + sparse).reshape(orig_shape)
    x = x + _L0_xattn_ref(_layernorm(x, axis=-1), ctx_2048, L0_xattn_Wq, L0_xattn_Wk, L0_xattn_Wv)
    x = x + _L0_attn_ref(_layernorm(x, axis=-1), L0_attn_w_q, L0_attn_b_q, L0_attn_w_k, L0_attn_b_k, L0_attn_w_v, L0_attn_b_v, L0_attn_w_o, L0_attn_b_o)
    x = x + _L0_ffn_ref(_layernorm(x, axis=-1), L0_ffn_w1, L0_ffn_w3, L0_ffn_w2)
    x = x + _L1_xattn_ref(_layernorm(x, axis=-1), ctx_2048, L1_xattn_decay, L1_xattn_W_in, L1_xattn_b_in, L1_xattn_W_out, L1_xattn_b_out, L1_xattn_gamma, L1_xattn_beta)
    x = x + _L1_attn_ref(_layernorm(x, axis=-1), L1_attn_W_mem, L1_attn_conv_k, L1_attn_W_q, L1_attn_theta, L1_attn_decay_slopes, L1_attn_anchor_slopes, L1_attn_score_scale, L1_attn_W_re, L1_attn_W_im, L1_attn_norm_scale, L1_attn_W_out)
    x = x + _L1_ffn_ref(_layernorm(x, axis=-1), L1_ffn_gate_w, L1_ffn_expert_gate_up, L1_ffn_expert_down, L1_ffn_shared_gate_up, L1_ffn_shared_down, L1_ffn_shared_gate_vec)
    return x

_drawn_inputs = setup_inputs


def setup_inputs(seed=0):
    import zlib

    import numpy as np

    out = dict(_drawn_inputs(seed))
    spreads = {'L0_attn_b_q': (0.0, 2.0),
     'L0_attn_b_k': (0.0, 2.0),
     'L0_attn_b_v': (0.0, 0.8),
     'L0_attn_b_o': (0.0, 0.1),
     'L1_xattn_b_in': (0.0, 0.1),
     'L1_xattn_b_out': (0.0, 0.1),
     'L1_xattn_gamma': (1.0, 0.2),
     'L1_xattn_beta': (0.0, 0.1),
     'L1_attn_score_scale': (1.0, 0.6),
     'L1_attn_norm_scale': (1.0, 0.2)}
    factors = {'L0_attn_w_q': 64.0,
     'L0_attn_w_k': 64.0,
     'L0_attn_w_v': 23.699,
     'L0_attn_w_o': 8.0,
     'L1_attn_anchor_slopes': 33.992,
     'L1_ffn_gate_w': 8.0,
     'L1_ffn_expert_gate_up': 8.0,
     'L1_ffn_expert_down': 8.0,
     'L1_ffn_shared_gate_up': 8.0,
     'L1_ffn_shared_down': 8.0,
     'L1_ffn_shared_gate_vec': 8.0}
    for name, (base, spread) in spreads.items():
        noise = np.random.default_rng([zlib.crc32(name.encode()), seed]).standard_normal(out[name].shape)
        drawn = base * np.exp(spread * noise) if base else spread * noise
        out[name] = jnp.asarray(drawn.astype(out[name].dtype))
    for name, factor in factors.items():
        out[name] = (out[name] * factor).astype(out[name].dtype)
    return out
```

```python
from contextlib import ExitStack
import math

import concourse.bass as bass
from concourse import mybir

F32 = mybir.dt.float32
F16 = mybir.dt.float16
F32R = mybir.dt.float32r
U32 = mybir.dt.uint32
ALU = mybir.AluOpType
ACT = mybir.ActivationFunctionType
AX_X = mybir.AxisListType.X

P = 128
B, L, D = 2, 128, 256
KT = D // P
M = 2048
MB = M // P
NB = B * MB
XH, XD = 32, 8
GROUPS = XH // 4
ROUNDS = GROUPS // 2
CTX_SLOTS = V_SLOTS = P_SLOTS = 4
AH, AD = 16, 128
HID, HT_FFN = 682, 6
CK, CH, CM = 32, 8, 8
NF = CK * CH * CM
FT = NF // P
CONV = 4
SW = 48
E, TOPK, EI = 16, 4, 176
UNITS = E + 4
DT = 28
TWO_PI = 2.0 * math.pi
ARENA = 10048
ROUND_MAGIC = 1.5 * 2.0 ** 23


def build_program(nc, io, stop=9):
    ctx = ExitStack()
    with ctx:
        sems = {}

        def sem(name):
            if name not in sems:
                sems[name] = ctx.enter_context(nc.semaphore(name))
            return sems[name]

        def sb(name, shape, dt=F32):
            return ctx.enter_context(nc.sbuf_tensor("sb_" + name, shape, dt))

        ps = ctx.enter_context(nc.psum_tensor("ps", [P, 8, 512], F32))
        x = sb("x", [P, B, D])
        xn = sb("xn", [P, B, D])
        xnT = sb("xnT", [P, KT, B, 3 + L])
        bn = sb("bn", [P, B, 6])
        mv = sb("mv", [P, B, 2])
        lnv = sb("lnv", [P, B])
        rstd = sb("rstd", [P, B])
        id32 = sb("id32", [P, P])
        id16 = sb("id16", [P, P], F16)
        ones = sb("ones", [P, P])
        tri = sb("tri", [P, P])
        mask = sb("mask", [P, L])

        w_x = sb("w_x", [P, 3 * KT * D])
        w_xq = w_x[:, 0:KT * D].rearrange("p (k n) -> p k n", k=KT)
        w_xkv = w_x[:, KT * D:].rearrange("p (k n) -> p k n", k=KT)
        w_out2 = w_x[:].rearrange("p (t n) -> p t n", t=6)
        big = sb("big", [P, 3 * KT * 2048 + 1792])
        w_qkv = big[:, 0:3 * KT * 2048].rearrange("p (s k n) -> p s k n", s=3, k=KT)
        w_gu = big[:, 0:KT * UNITS * 2 * EI].rearrange("p (k n) -> p k n", k=KT)
        mid = sb("mid", [P, AH * D + 3 * HT_FFN * D])
        w_o = mid[:, 0:AH * D].rearrange("p (h n) -> p h n", h=AH)
        w_ffn = mid[:, AH * D:].rearrange("p (w n) -> p w n", w=3)
        w_cm = mid[:, 0:KT * CONV * 288].rearrange("p (k w n) -> p k w n", k=KT, w=CONV)
        w_down = mid[:, 0:DT * D].rearrange("p (t n) -> p t n", t=DT)
        b_qkv = sb("b_qkv", [P, 3, AH])
        b_o = sb("b_o", [P, D])
        w_in = sb("w_in", [P, KT, D])
        w_out1 = sb("w_out1", [P, KT, D])
        b_in = sb("b_in", [P, KT])
        vecs = sb("vecs", [P, 3, D])
        decay = sb("decay", [P, 1])
        w_mem = sb("w_mem", [P, KT, 288])
        w_conv = sb("w_conv", [P, CONV, 288])
        w_q4 = sb("w_q4", [P, KT, 1024])
        w_ri = sb("w_ri", [P, 2, FT, 96])
        w_nrm = sb("w_nrm", [P, FT])
        small = sb("small", [P, 4, 32])
        w_rt = sb("w_rt", [P, KT, 17])
        iota = sb("iota", [P, E])

        theta = sb("theta", [P, NF])
        geo = w_q4[:].rearrange("p k n -> p (k n)")
        accs = theta[:].rearrange("p (b n) -> p b n", b=B)

        qraw = accs[:, 1, 0:512].rearrange("p (b n) -> p b n", b=B)
        qpack = accs[:, 0].bitcast(F16).rearrange("p (b n) -> p b n", b=B)
        qsq = accs[:, 1, 512:1024].rearrange("p (b n) -> p b n", b=B)
        qms = sb("qms", [P, B, XH])
        qrs = sb("qrs", [P, B, XH])

        arena = sb("arena", [P, ARENA])

        def cut(start, n):
            return arena[:, start:start + n]

        halves = sb("halves", [P, 3840], F32R)
        wkv_half = halves[:, 0:2048].rearrange("p (c k n) -> p c k n", c=2, k=KT)
        ctx_half = halves[:, 2048:3072].rearrange("p (s c k m) -> p s c k m", s=2, c=2, k=KT)
        HALF_PRODUCTS = ((0, 0), (1, 0), (0, 1))

        o = 0
        ctxT = cut(o, 4 * 256).rearrange("p (s k m) -> p s k m", s=4, k=KT); o += 1024
        kraw = cut(o, 512).rearrange("p (s n) -> p s n", s=2); o += 512
        kms = cut(o, 64).rearrange("p (s n) -> p s n", s=2); o += 64
        krs = cut(o, 64).rearrange("p (s n) -> p s n", s=2); o += 64
        kln = cut(o, 32); o += 32
        kn = cut(o, 256); o += 256
        kpack = cut(o, 1024).bitcast(F16).rearrange("p (s n) -> p s n", s=2); o += 1024
        kT = cut(o, 1024).bitcast(F16).rearrange("p (s g m) -> p s g m", s=2, g=GROUPS); o += 1024
        v_sb = cut(o, 4 * 288).rearrange("p (s h c) -> p s h c", s=4, h=XH); o += 1152
        probs = cut(o, 4096).rearrange("p (s a g j n) -> p s a g j n", s=4, a=2, g=2, j=2); o += 4096
        ksq = big[:, 12288:12800].rearrange("p (s n) -> p s n", s=2)
        gprod = big[:, 12800:13312].rearrange("p (s k m) -> p s k m", s=2, k=KT)
        uacc = big[:, 13312:13824].rearrange("p (b k m) -> p b k m", b=B, k=KT)
        qbd = w_ri[:].rearrange("p c t n -> p (c t n)")[:, 0:2048].bitcast(F16).rearrange(
            "p (b g n) -> p b g n", b=B, g=GROUPS)
        zer = cut(o, 256).bitcast(F16); o += 256
        rden = cut(o, 64).rearrange("p (b h) -> p b h", b=B); o += 64
        assert o <= ARENA, o
        dec = sb("dec", [P, 4])
        usum = sb("usum", [P, KT, B])
        gsum = sb("gsum", [P, 1])
        smean = sb("smean", [P, KT, B])
        bg = sb("bg", [P, KT])
        pw = sb("pw", [P, B, 32])
        logw = sb("logw", [P, 6, 32])
        iden = sb("iden", [P, B, 32])


        eng_programs = {}

        loads = [
            ("w_attn", w_qkv[:, 0], io["w_q"]), ("w_attn", w_qkv[:, 1], io["w_k"]),
            ("w_attn", w_qkv[:, 2], io["w_v"]), ("w_attn", w_o, io["w_o"]),
            ("w_attn", b_qkv[:], io["b_qkv"]), ("w_attn", b_o[:], io["b_o"]),
            ("w_attn", mask[:], io["mask"]),
            ("w_ffn", w_ffn, io["w_ffn"]),
            ("w_sum", w_in[:], io["w_in"]), ("w_sum", w_out1[:], io["w_out1"]),
            ("w_sum", b_in[:], io["b_in"]), ("w_sum", vecs[:], io["vecs"]),
            ("w_phase", w_mem[:], io["w_mem"]), ("w_phase", w_conv[:], io["w_conv"]),
            ("w_phase", w_nrm[:], io["w_nrm"]), ("w_phase", small[:, 0:3], io["small"]),
            ("w_phase", tri[:], io["tri"]),
            ("w_moe", w_rt[:], io["w_rt"]), ("w_moe", iota[:], io["iota"]),
        ]
        loaded = {}
        for name, _, _ in loads:
            loaded[name] = loaded.get(name, 0) + 16
        block = ctx.enter_context(nc.Block())

        LN_OF = {"xattn": 0, "attn": 1, "ffn": 2, "summary": 3, "summary2": 4, "phase": 5, "moe": 6}

        @block.sync
        def _(sp):
            sp.dma_start(x[:], io["x"].rearrange("b l d -> l b d")).then_inc(sem("x_loaded"), 16)
            sp.dma_start(id32[:], io["id32"]).then_inc(sem("x_loaded"), 16)
            sp.dma_start(w_xq, io["w_xq"]).then_inc(sem("wq_loaded"), 16)
            sp.dma_start(w_xkv, io["w_xkv"]).then_inc(sem("w_x"), 16)
            for s in range(CTX_SLOTS):
                sp.dma_start(ctxT[:, s], io["ctx"][s]).then_inc(sem(f"ctx_loaded{s}"), 16)
                if s == 0:
                    sp.dma_start(id16[:], io["id16"]).then_inc(sem("w_x"), 16)
            sp.dma_start(decay[:], io["decay"]).then_inc(sem("decay_loaded"), 16)
            with sp.Fori(1, NB // 4) as q:
                for s in range(CTX_SLOTS):
                    sp.wait_ge(sem("ctx_split"), 4 * q + (s - 3))
                    sp.wait_ge(sem("ctx_weighted"), 4 * q + (s - 3))
                    sp.dma_start(ctxT[:, s], io["ctx"][bass.ds(4 * q + s, 1)].rearrange("o p k m -> p (o k) m")
                                 ).then_inc(sem(f"ctx_loaded{s}"), 16)
            if stop >= 4:
                sp.wait_ge(sem("ctx_weighted"), NB)
                sp.wait_ge(sem("u_ready"), 1)
                sp.dma_start(w_ri[:], io["w_ri"]).then_inc(sem("w_ri_loaded"), 16)
                sp.dma_start(w_out2, io["w_out2"]).then_inc(sem("late_loaded"), 16)
                sp.dma_start(w_q4[:], io["w_q4"]).then_inc(sem("late_loaded"), 16)
                sp.wait_ge(sem("acc_transposed"), B)
                sp.dma_start(theta[:], io["theta"]).then_inc(sem("late_loaded"), 16)
            if stop >= 5:
                sp.wait_ge(sem("qk_projected"), AH)
                sp.wait_ge(sem("v_projected"), 2 * AH // 4)
                for k in range(KT):
                    sp.dma_start(w_gu[:, k], io["w_gu"][k]).then_inc(sem("gu_loaded"), 16)
            if stop >= 5:
                sp.wait_ge(sem("y_gated"), B * 4)
                sp.dma_start(w_down, io["w_down"]).then_inc(sem("down_loaded"), 16)
            if stop < 5:
                for name, n in loaded.items():
                    sp.wait_ge(sem(name), n)
                if stop >= 4: sp.wait_ge(sem("late_loaded"), 48)
            sp.wait_ge(sem("x_final"), B)
            sp.dma_start(io["out"].rearrange("b l d -> l b d"), x[:]).then_inc(sem("stored"), 16)
            sp.wait_ge(sem("stored"), 16)

        qT = cut(0, 512).rearrange("p (s n) -> p s n", s=2)
        kT2 = cut(512, 512).rearrange("p (s n) -> p s n", s=2)
        v_at = cut(1024, 2 * 2 * 512).rearrange("p (s b n) -> p s b n", s=2, b=B)
        s_at = cut(3072, 512).rearrange("p (s b n) -> p s b n", s=2, b=B)
        p_at = cut(3584, 512).rearrange("p (s b n) -> p s b n", s=2, b=B)
        pT_at = cut(4096, 512).rearrange("p (s b n) -> p s b n", s=2, b=B)
        oT_at = cut(4608, AH * 256).rearrange("p (h n) -> p h n", h=AH)
        st_at = cut(8704, 32).rearrange("p (s k b) -> p s k b", s=2, k=8)
        tneg = cut(8736, 768)
        fsc = cut(9504, 16)
        silu_f = cut(0, 512).rearrange("p (s n) -> p s n", s=2)
        gT = cut(512, HT_FFN * 256).rearrange("p (t n) -> p t n", t=HT_FFN)
        smb = cut(9520, KT * B * P).rearrange("p (k b n) -> p k b n", k=KT, b=B)
        kv_z = cut(0, B * 288).rearrange("p (b c) -> p b c", b=B)
        turns = cut(576, 2 * B * 512).rearrange("p (s b f) -> p s b f", s=2, b=B)
        frac = mid[:, 0:2 * B * 512].rearrange("p (s b f) -> p s b f", s=2, b=B)
        cs = cut(2624, 2 * 2 * B * 512).rearrange("p (s c b f) -> p s c b f", s=2, c=2, b=B)
        yv = mid[:, 7168:8704].rearrange("p (b n) -> p b n", b=B)
        ysc = mid[:, 2304:3840].rearrange("p (s b k n) -> p s b k n", s=2, b=B, k=8)
        ysg = mid[:, 3840:4608].rearrange("p (s b k n) -> p s b k n", s=2, b=B, k=8)
        yT = cut(576, 6 * 256).rearrange("p (t n) -> p t n", t=6)
        sumo = cut(2048, B * D).rearrange("p (b n) -> p b n", b=B)
        xe_half = halves[:, 0:1024].rearrange("p (c k n) -> p c k n", c=2, k=KT)
        gu_half = halves[:, 1024:3840].rearrange("p (s c k n) -> p s c k n", s=2, c=2, k=KT)
        H = cut(0, B * UNITS * EI).rearrange("p (b n) -> p b n", b=B)
        HT = cut(7040, 4 * 512).rearrange("p (s t b n) -> p s t b n", s=4, t=2, b=B)
        esg = cut(9088, 4 * EI).rearrange("p (s n) -> p s n", s=4)
        lg = cut(9792, B * 17).rearrange("p (b n) -> p b n", b=B)
        ex = cut(9832, B * 17).rearrange("p (b n) -> p b n", b=B)
        lmax = cut(9870, 2)
        top = cut(9872, B * 8).rearrange("p (b n) -> p b n", b=B)
        topi = cut(9888, B * 8).bitcast(U32).rearrange("p (b n) -> p b n", b=B)
        topf = cut(9904, B * 8).rearrange("p (b n) -> p b n", b=B)
        eq = w_mem[:].rearrange("p k n -> p (k n)")[:, 0:B * TOPK * E].rearrange("p (b k n) -> p b k n", b=B, k=TOPK)
        cw = cut(9920, B * UNITS).rearrange("p (b n) -> p b n", b=B)
        cws = cut(9960, 2)
        msk = cut(9964, B * E).rearrange("p (b n) -> p b n", b=B)
        qf = cut(6720, 4 * 3 * 256).rearrange("p (q c n) -> p q c n", q=4, c=3)
        pa = mid[:, 4608:6656].rearrange("p (s h c n) -> p s h c n", s=2, h=2, c=2)

        def ln_stats(dve, k):
            src = xn if k == LN_OF["summary2"] else x
            for b in range(B):
                step(dve, nc.vector.bn_stats(bn[:, b], src[:, b]))
            for b in range(B):
                i = nc.vector.bn_aggr(mv[:, b], bn[:, b])
                if b == B - 1:
                    i.then_inc(sem("ln_stats"), 1)
            dve.wait_ge(sem("ln_rstd"), k + 1)
            for b in range(B):
                nc.vector.tensor_scalar(xn[:, b], src[:, b], mv[:, b, 0:1], rstd[:, b:b + 1], ALU.subtract,
                                        ALU.mult).then_inc(sem("ln_normed"), 1)

        def ln_copy(dve, n, bank):
            dve.wait_ge(sem("ln_transposed"), n + 1)
            nc.vector.tensor_copy(xnT[:, :, :, 3:], ps[:, bank].rearrange("p (k b l) -> p k b l", k=KT, b=B)
                                  ).then_inc(sem("xnT_ready"), 1)

        def ln_rstd(act, k):
            act.wait_ge(sem("ln_stats"), k + 1)
            nc.scalar.activation(lnv[:], mv[:, :, 1], ACT.Ln, bias=1e-5).then_inc(sem("ln_log"), 1)
            act.wait_ge(sem("ln_log"), k + 1)
            nc.scalar.activation(rstd[:], lnv[:], ACT.Exp, scale=-0.5).then_inc(sem("ln_rstd"), 1)

        def ln_transpose(pe, k, bank):
            pe.wait_ge(sem("ln_normed"), B * (k + 1))
            for kt in range(KT):
                for b in range(B):
                    i = nc.tensor.transpose(ps[:, bank, (kt * B + b) * P:(kt * B + b + 1) * P],
                                            xn[:, b, kt * P:(kt + 1) * P], id32[:])
            i.then_inc(sem("ln_transposed"), 1)

        steps = [0]

        def step(dve, ins):
            steps[0] += 1
            ins.then_inc(sem("dve_step"), 1)
            dve.wait_ge(sem("dve_step"), steps[0])


        def tensor_attention(pe):
            T = nc.tensor
            pe.wait_ge(sem("u_ready"), 1)
            for et in range(KT):
                for kt in range(KT):
                    i = T.matmul(ps[:, 6, et * B:et * B + B], w_in[:, kt, et * P:(et + 1) * P], usum[:, kt],
                                 start=(kt == 0), stop=(kt == KT - 1))
            i.then_inc(sem("state_summed"), 1)
            ln_transpose(pe, LN_OF["attn"], 7)
            pe.wait_ge(sem("xnT_ready"), 2)
            pe.wait_ge(sem("w_attn"), loaded["w_attn"])
            pe.wait_ge(sem("state_taken"), 1)
            for i in range(AH + 4):
                if i < AH and i % 4 == 0:
                    for b in range(B):
                        if i or b:
                            pe.wait_ge(sem("v_copied"), 2 * (i // 4) + b)
                        if i == 8:
                            pe.wait_ge(sem("ffn_scaled"), 1)
                        for kt in range(KT):
                            ins = T.matmul(ps[:, 2], xnT[:, kt, b, 3:], w_qkv[:, 2, kt, i * AD:(i + 4) * AD],
                                           start=(kt == 0), stop=(kt == KT - 1))
                        ins.then_inc(sem("v_projected"), 1)
                if i == 6:
                    pe.wait_ge(sem("v_copied"), 4)
                    pe.wait_ge(sem("ffn_abs"), 3)
                    pe.wait_ge(sem("ones_set"), 1)
                    T.matmul(ps[:, 2, 0:3], ones[:], fsc[:, 0:3], start=True, stop=True).then_inc(sem("ffn_summed"), 1)
                if i < AH:
                    if i >= 2:
                        pe.wait_ge(sem("qk_taken"), 2 * (i - 1))
                    for c in range(2):
                        for kt in range(KT):
                            ins = T.matmul(ps[:, i % 2, c * 256:c * 256 + 256], w_qkv[:, c, kt, i * AD:(i + 1) * AD],
                                           xnT[:, kt, :, 3:], start=(kt == 0), stop=(kt == KT - 1))
                    ins.then_inc(sem("qk_projected"), 1)
                h = i - 1
                if 0 <= h < AH:
                    pe.wait_ge(sem("qk_taken"), 2 * (h + 1))
                    if h:
                        pe.wait_ge(sem("s_masked"), h)
                    for b in range(B):
                        ins = T.matmul(ps[:, 3, b * P:b * P + P], qT[:, h % 2, b * P:b * P + P],
                                       kT2[:, h % 2, b * P:b * P + P], start=True, stop=True)
                    ins.then_inc(sem("s_scored"), 1)
                h = i - 2
                if 0 <= h < AH:
                    pe.wait_ge(sem("p_normed"), h + 1)
                    if h:
                        pe.wait_ge(sem("pT_taken"), h)
                    for b in range(B):
                        ins = T.transpose(ps[:, 4, b * P:b * P + P], p_at[:, h % 2, b], id32[:])
                    ins.then_inc(sem("p_turned"), 1)
                h = i - 3
                if 0 <= h < AH:
                    pe.wait_ge(sem("pT_taken"), h + 1)
                    pe.wait_ge(sem("v_copied"), 2 * (h // 4 + 1))
                    if h:
                        pe.wait_ge(sem("o_taken"), h)
                    for b in range(B):
                        ins = T.matmul(ps[:, 5, b * P:b * P + P], v_at[:, (h // 4) % 2, b, (h % 4) * AD:(h % 4 + 1) * AD],
                                       pT_at[:, h % 2, b], start=True, stop=True)
                    ins.then_inc(sem("o_summed"), 1)
                h = i - 4
                if 0 <= h < AH:
                    output_head(pe, h)
            

        def output_head(pe, h):
            pe.wait_ge(sem("o_taken"), h + 1)
            for b in range(B):
                ins = nc.tensor.matmul(ps[:, 6 + b, 0:D], oT_at[:, h, b * P:b * P + P], w_o[:, h],
                                       start=(h == 0), stop=(h == AH - 1))
            if h == AH - 1:
                ins.then_inc(sem("attn_out"), 1)

        def scalar_attention(act):
            ln_rstd(act, LN_OF["attn"])
            act.wait_ge(sem("w_phase"), loaded["w_phase"])
            nc.scalar.activation(logw[:, 0], small[:, 0], ACT.Abs).then_inc(sem("slope_step"), 1)
            act.wait_ge(sem("slope_step"), 1)
            nc.scalar.activation(logw[:, 1], logw[:, 0], ACT.Exp, scale=-1.0).then_inc(sem("slope_step"), 1)
            act.wait_ge(sem("slope_step"), 2)
            nc.scalar.activation(logw[:, 2], logw[:, 1], ACT.Ln, bias=1.0).then_inc(sem("slope_log"), 1)
            for i in range(AH + 2):
                if i < AH and i % 4 == 0:
                    for b in range(B):
                        act.wait_ge(sem("v_projected"), 2 * (i // 4) + b + 1)
                        if i >= 8:
                            act.wait_ge(sem("o_summed"), i - 4)
                        nc.scalar.copy(v_at[:, (i // 4) % 2, b], ps[:, 2]).then_inc(sem("v_copied"), 1)
                h = i - 1
                if 0 <= h < AH:
                    act.wait_ge(sem("s_negmax"), h + 1)
                    if h >= 2:
                        act.wait_ge(sem("p_turned"), h - 1)
                    for b in range(B):
                        nc.scalar.activation(p_at[:, h % 2, b], s_at[:, h % 2, b], ACT.Exp,
                                             bias=st_at[:, h % 2, 0, b:b + 1],
                                             accum_out=st_at[:, h % 2, 1, b:b + 1]).then_inc(sem("p_exp"), 1)
                h = i - 2
                if 0 <= h < AH:
                    act.wait_ge(sem("p_turned"), h + 1)
                    if h >= 2:
                        act.wait_ge(sem("o_summed"), h - 1)
                    nc.scalar.copy(pT_at[:, h % 2], ps[:, 4, 0:256].rearrange("p (b n) -> p b n", b=B)
                                   ).then_inc(sem("pT_taken"), 1)

        def vector_attention(dve):
            V = nc.vector
            ln_stats(dve, LN_OF["attn"])
            ln_copy(dve, 1, 7)
            dve.wait_ge(sem("state_summed"), 1)
            for et in range(KT):
                step(dve, V.tensor_scalar(smean[:, et], ps[:, 6, et * B:et * B + B], bg[:, et:et + 1], 1.0 / M,
                                          ALU.add, ALU.mult))
            V.tensor_copy(smb, smean[:, :, :, None].to_broadcast([P, KT, B, P])).then_inc(sem("state_taken"), 1)
            dve.wait_ge(sem("w_attn"), loaded["w_attn"])
            dve.wait_ge(sem("w_ffn"), loaded["w_ffn"])
            for i in range(AH + 3):
                h = i - 2
                if 0 <= h < AH:
                    dve.wait_ge(sem("p_exp"), 2 * (h + 1))
                    step(dve, V.reciprocal(st_at[:, h % 2, 2], st_at[:, h % 2, 1]))
                    V.tensor_tensor(p_at[:, h % 2], p_at[:, h % 2],
                                    st_at[:, h % 2, 2, :, None].to_broadcast([P, B, L]), ALU.mult
                                    ).then_inc(sem("p_normed"), 1)
                if i < AH:
                    dve.wait_ge(sem("qk_projected"), i + 1)
                    if i >= 2:
                        dve.wait_ge(sem("s_scored"), i - 1)
                    V.tensor_scalar(qT[:, i % 2], ps[:, i % 2, 0:256], b_qkv[:, 0, i:i + 1], AD ** -0.5, ALU.add,
                                    ALU.mult).then_inc(sem("qk_taken"), 1)
                    V.tensor_scalar(kT2[:, i % 2], ps[:, i % 2, 256:512], b_qkv[:, 1, i:i + 1], None, ALU.add
                                    ).then_inc(sem("qk_taken"), 1)
                h = i - 1
                if 0 <= h < AH:
                    dve.wait_ge(sem("s_scored"), h + 1)
                    if h >= 2:
                        dve.wait_ge(sem("p_exp"), 2 * (h - 1))
                    V.tensor_tensor(s_at[:, h % 2], ps[:, 3, 0:256].rearrange("p (b n) -> p b n", b=B),
                                    mask[:, None, :].to_broadcast([P, B, L]), ALU.add).then_inc(sem("s_masked"), 1)
                    dve.wait_ge(sem("s_masked"), h + 1)
                    V.tensor_reduce(st_at[:, h % 2, 0], s_at[:, h % 2], AX_X, ALU.max, negate=True
                                    ).then_inc(sem("s_negmax"), 1)
                h = i - 3
                if 0 <= h < AH:
                    dve.wait_ge(sem("o_summed"), h + 1)
                    V.tensor_scalar(oT_at[:, h], ps[:, 5, 0:256], b_qkv[:, 2, h:h + 1], None, ALU.add
                                    ).then_inc(sem("o_taken"), 1)
                if 2 <= i < 5:
                    V.tensor_reduce(fsc[:, i - 2:i - 1], w_ffn[:, i - 2], AX_X, ALU.add, apply_absolute_value=True
                                    ).then_inc(sem("ffn_abs"), 1)
                if i == 7:
                    dve.wait_ge(sem("ffn_summed"), 1)
                    V.tensor_scalar(fsc[:, 3:6], ps[:, 2, 0:3], 1.0 / (HID * D), None, ALU.mult).then_inc(sem("ffn_scaled"), 1)
                    dve.wait_ge(sem("ffn_scaled"), 1)
                    step(dve, V.tensor_scalar(fsc[:, 6:9], fsc[:, 3:6], 0.5, None, ALU.mult))
                    step(dve, V.tensor_scalar(fsc[:, 9:12], fsc[:, 3:6], -0.5, None, ALU.mult))
                if 8 <= i < 11:
                    w = w_ffn[:, i - 8]
                    for half in (w[:, 0:768], w[:, 768:1536]):
                        step(dve, V.tensor_scalar(tneg, half, fsc[:, i + 1:i + 2], None, ALU.is_lt))
                        step(dve, V.scalar_tensor_tensor(half, half, fsc[:, i - 2:i - 1], tneg, ALU.is_gt, ALU.subtract))
                    if i == 10:
                        V.tensor_copy(fsc[:, 15:16], fsc[:, 5:6]).then_inc(sem("ffn_ternary"), 1)
            dve.wait_ge(sem("slope_log"), 1)
            step(dve, V.tensor_scalar(logw[:, 3], small[:, 0], 0.0, None, ALU.max))
            step(dve, V.tensor_tensor(logw[:, 4], logw[:, 3], logw[:, 2], ALU.add))
            step(dve, V.tensor_tensor(logw[:, 5], logw[:, 4], small[:, 2], ALU.mult))
            dve.wait_ge(sem("attn_out"), 1)
            add_output(dve, [ps[:, 6, 0:D], ps[:, 7, 0:D]], stop == 1, bias=b_o[:])

        def add_output(dve, sums, final, bias=None, scale=None):
            for b in range(B):
                if scale is not None:
                    i = nc.vector.scalar_tensor_tensor(x[:, b], sums[b], scale, x[:, b], ALU.mult, ALU.add)
                else:
                    if bias is not None:
                        step(dve, nc.vector.tensor_tensor(x[:, b], x[:, b], bias, ALU.add))
                    i = nc.vector.tensor_tensor(x[:, b], x[:, b], sums[b], ALU.add)
                if final:
                    i.then_inc(sem("x_final"), 1)
                else:
                    step(dve, i)

        def tensor_ffn(pe):
            T = nc.tensor
            ln_transpose(pe, LN_OF["ffn"], 0)
            pe.wait_ge(sem("w_sum"), loaded["w_sum"])
            if stop > 2:
                for b in range(B):
                    for kt in range(KT):
                        i = T.matmul(ps[:, 7, b * D:(b + 1) * D], smb[:, kt, b], w_out1[:, kt], start=(kt == 0),
                                     stop=(kt == KT - 1))
                i.then_inc(sem("summary_ready"), 1)
            pe.wait_ge(sem("xnT_ready"), 3)
            pe.wait_ge(sem("ffn_ternary"), 1)
            for j in range(HT_FFN + 2):
                if j < HT_FFN:
                    if j >= 4:
                        pe.wait_ge(sem("g_ready"), j - 3)
                    for c in range(2):
                        for kt in range(KT):
                            i = T.matmul(ps[:, 1 + j % 4, c * 256:c * 256 + 256],
                                         w_ffn[:, c, kt * HT_FFN * P + j * P:kt * HT_FFN * P + (j + 1) * P],
                                         xnT[:, kt, :, 3:], start=(kt == 0), stop=(kt == KT - 1))
                    i.then_inc(sem("h_projected"), 1)
                t = j - 2
                if t >= 0:
                    pe.wait_ge(sem("g_ready"), t + 1)
                    for b in range(B):
                        i = T.matmul(ps[:, 5 + b, 0:D], gT[:, t, b * P:b * P + P], w_ffn[:, 2, t * D:(t + 1) * D],
                                     start=(t == 0), stop=(t == HT_FFN - 1))
            i.then_inc(sem("ffn_out"), 1)

        def scalar_ffn(act):
            ln_rstd(act, LN_OF["ffn"])
            nc.scalar.preload_act_table_set("silu_and_others")
            for j in range(HT_FFN):
                act.wait_ge(sem("h_projected"), j + 1)
                if j >= 2:
                    act.wait_ge(sem("g_ready"), j - 1)
                nc.scalar.activation(silu_f[:, j % 2], ps[:, 1 + j % 4, 0:256], ACT.Silu, scale=fsc[:, 3:4]
                                     ).then_inc(sem("h_gated"), 1)

        def vector_ffn(dve):
            V = nc.vector
            ln_stats(dve, LN_OF["ffn"])
            ln_copy(dve, 2, 0)
            if stop > 2:
                dve.wait_ge(sem("summary_ready"), 1)
                step(dve, V.tensor_tensor(sumo, ps[:, 7].rearrange("p (b n) -> p b n", b=B),
                                          vecs[:, 0:1, :].to_broadcast([P, B, D]), ALU.add))
            for j in range(HT_FFN):
                dve.wait_ge(sem("h_gated"), j + 1)
                V.scalar_tensor_tensor(gT[:, j], ps[:, 1 + j % 4, 256:512], fsc[:, 4:5], silu_f[:, j % 2], ALU.mult,
                                       ALU.mult).then_inc(sem("g_ready"), 1)
            dve.wait_ge(sem("ffn_out"), 1)
            add_output(dve, [ps[:, 5, 0:D], ps[:, 6, 0:D]], stop == 2, scale=fsc[:, 5:6])

        def vector_summary(dve):
            V = nc.vector
            ln_stats(dve, LN_OF["summary"])
            dve.wait_ge(sem("ln_normed"), B * (LN_OF["summary"] + 1))
            step(dve, V.tensor_tensor(xn[:], xn[:], sumo, ALU.add))
            ln_stats(dve, LN_OF["summary2"])
            dve.wait_ge(sem("ln_normed"), B * (LN_OF["summary2"] + 1))
            step(dve, V.tensor_tensor(xn[:], xn[:], vecs[:, 1:2, :].to_broadcast([P, B, D]), ALU.mult))
            step(dve, V.tensor_tensor(xn[:], xn[:], vecs[:, 2:3, :].to_broadcast([P, B, D]), ALU.add))
            add_output(dve, [xn[:, 0], xn[:, 1]], stop == 3)

        def tensor_phase(pe):
            T = nc.tensor
            ln_transpose(pe, LN_OF["phase"], 0)
            pe.wait_ge(sem("xnT_ready"), 4)
            pe.wait_ge(sem("w_cm_ready"), KT)
            for b in range(B):
                for n, (kt, w) in enumerate((kt, w) for kt in range(KT) for w in range(CONV)):
                    i = T.matmul(ps[:, 1 + b, 0:288], xnT[:, kt, b, w:w + L], w_cm[:, kt, w], start=(n == 0),
                                 stop=(n == KT * CONV - 1))
                i.then_inc(sem("z_ready"), 1)
            pe.wait_ge(sem("late_loaded"), 48)
            for kq in range(4):
                for c in range(2):
                    for kt in range(KT):
                        i = T.matmul(ps[:, 3 + kq, c * 256:c * 256 + 256],
                                     w_q4[:, kt, (2 * kq + c) * P:(2 * kq + c + 1) * P], xnT[:, kt, :, 3:],
                                     start=(kt == 0), stop=(kt == KT - 1))
                i.then_inc(sem("q4_projected"), 1)
            pe.wait_ge(sem("pw_ready"), 1)
            T.matmul(ps[:, 7, 0:B * 32], tri[:], pw[:].rearrange("p b k -> p (b k)"), start=True, stop=True
                     ).then_inc(sem("den_summed"), 1)
            pe.wait_ge(sem("z_taken"), B)
            pe.wait_ge(sem("q4_taken"), 8)
            pe.wait_ge(sem("w_ri_ready"), 2)
            for j in range(FT + 1):
                if j < FT:
                    kq, jj = j // 4, j % 4
                    pe.wait_ge(sem("re_weighted"), kq + 1)
                    pe.wait_ge(sem("im_weighted"), kq + 1)
                    if j >= 2:
                        pe.wait_ge(sem("state_used"), 2 * (j - 1))
                    for c in range(2):
                        for b in range(B):
                            i = T.matmul(ps[:, 1 + j % 2, (c * B + b) * P:(c * B + b + 1) * P],
                                         cs[:, kq % 2, c, b, jj * P:(jj + 1) * P], tri[:], start=True, stop=True)
                    i.then_inc(sem("state_ready"), 1)
                t = j - 1
                if t >= 0:
                    kq, jj = t // 4, t % 4
                    pe.wait_ge(sem("out_re"), t + 1)
                    pe.wait_ge(sem("out_im"), t + 1)
                    if jj == 0 and kq >= 2:
                        pe.wait_ge(sem("y_scaled"), B * (kq - 1))
                    for b in range(B):
                        for c in range(2):
                            i = T.matmul(ps[:, 3 + 2 * (kq % 2) + b, jj * 96:jj * 96 + 96],
                                         pa[:, t % 2, c, 0, b * P:b * P + P], w_ri[:, c, t], start=(c == 0), stop=(c == 1))
                    i.then_inc(sem("y_summed"), 1)
            for b in range(B):
                pe.wait_ge(sem("y_gated"), 3 * B + b + 1)
            pe.wait_ge(sem("state_used"), 2 * FT)
            for t in range(3):
                for u in range(2):
                    for b in range(B):
                        i = T.transpose(ps[:, [0, 1, 7][t], (u * B + b) * P:(u * B + b + 1) * P],
                                        yv[:, b, (2 * t + u) * P:(2 * t + u + 1) * P], id32[:])
                i.then_inc(sem("y_turned"), 1)
            for t in range(6):
                pe.wait_ge(sem("yT_taken"), t // 2 + 1)
                for b in range(B):
                    i = T.matmul(ps[:, 5 + b, 0:D], yT[:, t, b * P:b * P + P], w_out2[:, t], start=(t == 0), stop=(t == 5))
            i.then_inc(sem("phase_out"), 1)

        def vector_phase(dve):
            V = nc.vector
            ln_stats(dve, LN_OF["phase"])
            ln_copy(dve, 3, 0)
            for b in range(B):
                dve.wait_ge(sem("z_ready"), b + 1)
                V.tensor_copy(kv_z[:, b], ps[:, 1 + b, 0:288]).then_inc(sem("z_taken"), 1)
            dve.wait_ge(sem("z_taken"), B)
            step(dve, V.tensor_tensor(pw[:], kv_z[:, :, 256:288], small[:, 1:2, :].to_broadcast([P, B, 32]), ALU.mult))
            step(dve, V.tensor_scalar(pw[:], pw[:], 20.0, -20.0, ALU.min, ALU.max))
            V.tensor_tensor(pw[:], pw[:], logw[:, 5:6, :].to_broadcast([P, B, 32]), ALU.add).then_inc(sem("logp_ready"), 1)

            def angles(kq):
                s = kq % 2
                for b in range(B):
                    i = V.scalar_tensor_tensor(turns[:, s, b].rearrange("p (k m) -> p k m", m=CM),
                                               kv_z[:, b, kq * 64:kq * 64 + 64, None].to_broadcast([P, 64, CM]),
                                               1.0 / TWO_PI,
                                               theta[:, kq * 512:kq * 512 + 512].rearrange("p (k m) -> p k m", m=CM),
                                               ALU.mult, ALU.mult)
                step(dve, i)
                step(dve, V.tensor_scalar(frac[:, s], turns[:, s], ROUND_MAGIC, ROUND_MAGIC, ALU.add, ALU.subtract))
                V.tensor_tensor(frac[:, s], turns[:, s], frac[:, s], ALU.subtract).then_inc(sem("frac_ready"), 1)

            def weigh(kq):
                s = kq % 2
                dve.wait_ge(sem("cos_ready"), kq + 1)
                r = cs[:, s, 0].rearrange("p b (k n) -> p b k n", n=64)
                V.tensor_tensor(r, r, pw[:, :, kq * 8:kq * 8 + 8, None].to_broadcast([P, B, 8, 64]), ALU.mult
                                ).then_inc(sem("re_weighted"), 1)

            def scale_y(kq):
                dve.wait_ge(sem("y_summed"), 4 * kq + 4)
                for b in range(B):
                    V.tensor_tensor(ysc[:, kq % 2, b], ps[:, 3 + 2 * (kq % 2) + b, 0:384].rearrange("p (k n) -> p k n", n=SW),
                                    iden[:, b, kq * 8:kq * 8 + 8, None].to_broadcast([P, 8, SW]), ALU.mult
                                    ).then_inc(sem("y_scaled"), 1)

            def gate_y(kq):
                dve.wait_ge(sem("y_silu"), kq + 1)
                for b in range(B):
                    V.tensor_tensor(yv[:, b, kq * 192:kq * 192 + 192].rearrange("p (k n) -> p k n", n=24),
                                    ysc[:, kq % 2, b, :, 0:24], ysg[:, kq % 2, b], ALU.mult).then_inc(sem("y_gated"), 1)

            dve.wait_ge(sem("late_loaded"), 48)
            angles(0)
            angles(1)
            dve.wait_ge(sem("den_summed"), 1)
            step(dve, V.tensor_scalar(iden[:], ps[:, 7, 0:B * 32].rearrange("p (b k) -> p b k", b=B), 1e-4, None, ALU.max))
            step(dve, V.reciprocal(iden[:], iden[:]))
            weigh(0)
            for j in range(FT):
                kq, jj = j // 4, j % 4
                if jj == 0 and kq < 3:
                    if kq + 2 < 4:
                        dve.wait_ge(sem("cos_ready"), kq + 1)
                        angles(kq + 2)
                dve.wait_ge(sem("state_ready"), j + 1)
                if j >= 2:
                    dve.wait_ge(sem("y_summed"), j - 1)
                for c in range(2):
                    V.tensor_tensor(pa[:, j % 2, c], ps[:, 1 + j % 2].rearrange("p (c n) -> p c n", c=2),
                                    qf[:, kq, c:c + 2], ALU.mult).then_inc(sem("state_used"), 1)
                if jj == 1 and kq < 3:
                    weigh(kq + 1)
                if jj == 2 and kq:
                    scale_y(kq - 1)
                if jj == 3 and kq:
                    gate_y(kq - 1)
            scale_y(3)
            gate_y(3)
            for t in range(3):
                dve.wait_ge(sem("y_turned"), t + 1)
                V.tensor_copy(yT[:, 2 * t:2 * t + 2], ps[:, [0, 1, 7][t]].rearrange("p (u n) -> p u n", u=2)
                              ).then_inc(sem("yT_taken"), 1)
            dve.wait_ge(sem("phase_out"), 1)
            add_output(dve, [ps[:, 5, 0:D], ps[:, 6, 0:D]], stop == 4)

        def scalar_phase(act):
            ln_rstd(act, LN_OF["phase"])
            act.wait_ge(sem("logp_ready"), 1)
            nc.scalar.activation(pw[:], pw[:], ACT.Exp).then_inc(sem("pw_ready"), 1)

            def waves(kq):
                s = kq % 2
                act.wait_ge(sem("frac_ready"), kq + 1)
                if kq >= 2:
                    act.wait_ge(sem("state_ready"), 4 * (kq - 1))
                nc.scalar.activation(cs[:, s, 1], frac[:, s], ACT.Sin, scale=TWO_PI).then_inc(sem("sin_ready"), 1)
                nc.scalar.activation(turns[:, s], frac[:, s], ACT.Abs).then_inc(sem("abs_ready"), 1)
                act.wait_ge(sem("abs_ready"), kq + 1)
                nc.scalar.activation(cs[:, s, 0], turns[:, s], ACT.Sin, scale=-TWO_PI, bias=math.pi / 2
                                     ).then_inc(sem("cos_ready"), 1)

            def silu_y(kq):
                act.wait_ge(sem("y_scaled"), B * (kq + 1))
                nc.scalar.activation(ysg[:, kq % 2], ysc[:, kq % 2, :, :, 24:48], ACT.Silu).then_inc(sem("y_silu"), 1)

            nc.scalar.preload_act_table_set("silu_and_others")
            waves(0)
            for kq in range(4):
                act.wait_ge(sem("q4_projected"), kq + 1)
                nc.scalar.copy(qf[:, kq, 0:2], ps[:, 3 + kq].rearrange("p (c n) -> p c n", c=2)).then_inc(sem("q4_taken"), 1)
                nc.scalar.copy(qf[:, kq, 2], ps[:, 3 + kq, 0:256]).then_inc(sem("q4_taken"), 1)
            waves(1)
            waves(2)
            silu_y(0)
            waves(3)
            for kq in range(1, 4):
                silu_y(kq)
            nc.scalar.preload_act_table_set("natural_log_exp_and_others")

        def pool_phase(pool):
            G = nc.gpsimd
            def weigh(kq):
                pool.wait_ge(sem("sin_ready"), kq + 1)
                if kq == 0:
                    pool.wait_ge(sem("pw_ready"), 1)
                r = cs[:, kq % 2, 1].rearrange("p b (k n) -> p b k n", n=64)
                G.tensor_tensor(r, r, pw[:, :, kq * 8:kq * 8 + 8, None].to_broadcast([P, B, 8, 64]), ALU.mult
                                ).then_inc(sem("im_weighted"), 1)
            weigh(0)
            for j in range(FT):
                pool.wait_ge(sem("state_used"), 2 * j + 2)
                G.tensor_tensor(pa[:, j % 2, 0, 0], pa[:, j % 2, 0, 0], pa[:, j % 2, 0, 1], ALU.add
                                ).then_inc(sem("out_re"), 1)
                G.tensor_tensor(pa[:, j % 2, 1, 0], pa[:, j % 2, 1, 1], pa[:, j % 2, 1, 0], ALU.subtract
                                ).then_inc(sem("out_im"), 1)
                if j % 4 == 1 and j // 4 < 3:
                    weigh(j // 4 + 1)

        def tensor_experts(pe):
            T = nc.tensor
            ln_transpose(pe, LN_OF["moe"], 0)
            pe.wait_ge(sem("xnT_ready"), 5)
            pe.wait_ge(sem("w_moe"), loaded["w_moe"])
            for b in range(B):
                for kt in range(KT):
                    i = T.matmul(ps[:, 1, b * 32:b * 32 + 17], xnT[:, kt, b, 3:], w_rt[:, kt], start=(kt == 0),
                                 stop=(kt == KT - 1))
            i.then_inc(sem("routed"), 1)
            pe.wait_ge(sem("xe_split"), 1)
            turned = 0
            summed = 0

            def turn(n):
                last = min(DT, 2 * n + 2) - 1
                need = (min(UNITS * EI, (last + 1) * P) - 1) // EI + 1
                pe.wait_ge(sem("h_ready"), B * need)
                if n >= 2:
                    pe.wait_ge(sem("HT_taken"), n - 1)
                for u in range(2):
                    w = min(P, UNITS * EI - (2 * n + u) * P)
                    for b in range(B):
                        i = T.transpose(ps[0:w, 6 + n % 2, (u * B + b) * P:(u * B + b + 1) * P],
                                        H[:, b, (2 * n + u) * P:(2 * n + u) * P + w], id32[:])
                i.then_inc(sem("H_turned"), 1)

            def down(n):
                pe.wait_ge(sem("HT_taken"), n + 1)
                if n == 0:
                    pe.wait_ge(sem("down_loaded"), 16)
                    pe.wait_ge(sem("logits_taken"), 1)
                for u in range(2):
                    t = 2 * n + u
                    w = min(P, UNITS * EI - t * P)
                    for b in range(B):
                        i = T.matmul(ps[:, b, 0:D], HT[0:w, n % 4, u, b], w_down[0:w, t], start=(t == 0), stop=(t == DT - 1))
                i.then_inc(sem("downed"), 1)

            for k in range(B * UNITS):
                u, b = k // B, k % B
                if k >= 4:
                    pe.wait_ge(sem("h_ready"), k - 3)
                if b == 0:
                    pe.wait_ge(sem("gu_low"), u + 1)
                for n, (c, d) in enumerate(HALF_PRODUCTS):
                    for kt in range(KT):
                        i = T.matmul(ps[:, 2 + k % 4, 0:2 * EI], xe_half[:, c, kt, b * P:b * P + P], gu_half[:, u % 2, d, kt],
                                     start=(n + kt == 0), stop=(n == 2 and kt == KT - 1))
                i.then_inc(sem("gu_projected"), 1)
                if b == B - 1:
                    while turned < DT // 2 and (2 * turned + 2) * P <= (u - 1) * EI:
                        turn(turned)
                        turned += 1
                        if turned >= 2:
                            down(summed)
                            summed += 1
            while turned < DT // 2:
                turn(turned)
                turned += 1
                down(summed)
                summed += 1
            while summed < DT // 2:
                down(summed)
                summed += 1

        def unit_high(act, u):
            if u >= 2:
                act.wait_ge(sem("gu_projected"), B * (u - 1))
            nc.scalar.copy(gu_half[:, u % 2, 0], w_gu[:, :, u * 2 * EI:(u + 1) * 2 * EI]).then_inc(sem("gu_high"), 1)

        def pool_experts(pool):
            for u in range(UNITS):
                pool.wait_ge(sem("gu_high"), u + 1)
                nc.gpsimd.tensor_tensor(gu_half[:, u % 2, 1], w_gu[:, :, u * 2 * EI:(u + 1) * 2 * EI],
                                        gu_half[:, u % 2, 0].bitcast(F32), ALU.subtract).then_inc(sem("gu_low"), 1)

        def scalar_experts(act):
            act.wait_ge(sem("gu_loaded"), 16 * KT)
            for u in range(2):
                unit_high(act, u)
            ln_rstd(act, LN_OF["moe"])
            act.wait_ge(sem("lg_shifted"), 1)
            nc.scalar.activation(ex[:, :, 0:16], ex[:, :, 0:16], ACT.Exp).then_inc(sem("routes_exp"), 1)
            nc.scalar.activation(ex[:, :, 16:17], lg[:, :, 16:17], ACT.Exp, scale=-1.0).then_inc(sem("routes_exp"), 1)
            nc.scalar.preload_act_table_set("silu_and_others")
            evac = 0
            for k in range(B * UNITS):
                act.wait_ge(sem("gu_projected"), k + 1)
                if k >= 4:
                    act.wait_ge(sem("h_ready"), k - 3)
                nc.scalar.activation(esg[:, k % 4], ps[:, 2 + k % 4, 0:EI], ACT.Silu).then_inc(sem("g_gated"), 1)
                if k % B == B - 1:
                    u = k // B
                    if u + 2 < UNITS:
                        unit_high(act, u + 2)
                    while evac < DT // 2 and (2 * evac + 2) * P <= (u - 1) * EI:
                        take_H(act, evac)
                        evac += 1
            while evac < DT // 2:
                take_H(act, evac)
                evac += 1

        def take_H(act, n):
            act.wait_ge(sem("H_turned"), n + 1)
            if n >= 4:
                act.wait_ge(sem("downed"), n - 3)
            if n < DT // 2 - 1:
                nc.scalar.copy(HT[:, n % 4].rearrange("p t b n -> p (t b n)"), ps[:, 6 + n % 2]).then_inc(sem("HT_taken"), 1)
            else:
                w = UNITS * EI - (DT - 1) * P
                nc.scalar.copy(HT[:, n % 4, 0].rearrange("p b n -> p (b n)"), ps[:, 6 + n % 2, 0:256]
                               ).then_inc(sem("HT_last"), 1)
                nc.scalar.copy(HT[0:w, n % 4, 1].rearrange("p b n -> p (b n)"), ps[0:w, 6 + n % 2, 256:512]
                               ).then_inc(sem("HT_taken"), 1)

        def vector_experts(dve):
            V = nc.vector
            ln_stats(dve, LN_OF["moe"])
            ln_copy(dve, 4, 0)
            step(dve, V.tensor_copy(xe_half[:, 0], ps[:, 0].rearrange("p (k n) -> p k n", k=KT)))
            V.tensor_tensor(xe_half[:, 1], ps[:, 0].rearrange("p (k n) -> p k n", k=KT), xe_half[:, 0].bitcast(F32),
                            ALU.subtract).then_inc(sem("xe_split"), 1)
            dve.wait_ge(sem("routed"), 1)
            V.tensor_copy(lg, ps[:, 1, 0:64].rearrange("p (b n) -> p b n", b=B)[:, :, 0:17]).then_inc(sem("logits_taken"), 1)
            dve.wait_ge(sem("logits_taken"), 1)
            step(dve, V.tensor_reduce(lmax, lg[:, :, 0:16], AX_X, ALU.max))
            V.tensor_tensor(ex[:, :, 0:16], lg[:, :, 0:16], lmax[:, :, None].to_broadcast([P, B, 16]), ALU.subtract
                            ).then_inc(sem("lg_shifted"), 1)
            dve.wait_ge(sem("routes_exp"), 2)
            for b in range(B):
                step(dve, V.max(top[:, b], ex[:, b, 0:16]))
                step(dve, V.max_index(topi[:, b], top[:, b], ex[:, b, 0:16]))
            step(dve, V.tensor_copy(topf, topi))
            step(dve, V.tensor_tensor(eq, iota[:, None, None, :].to_broadcast([P, B, TOPK, E]),
                                      topf[:, :, 0:TOPK, None].to_broadcast([P, B, TOPK, E]), ALU.is_equal))
            step(dve, V.tensor_reduce(msk, eq.rearrange("p b k n -> p b n k"), AX_X, ALU.add))
            step(dve, V.tensor_tensor(msk, msk, ex[:, :, 0:16], ALU.mult))
            step(dve, V.tensor_reduce(cws, msk, AX_X, ALU.add))
            step(dve, V.reciprocal(cws, cws))
            step(dve, V.tensor_tensor(cw[:, :, 0:E], msk, cws[:, :, None].to_broadcast([P, B, E]), ALU.mult))
            step(dve, V.tensor_scalar(ex[:, :, 16:17], ex[:, :, 16:17], 1.0, None, ALU.add))
            step(dve, V.reciprocal(ex[:, :, 16:17], ex[:, :, 16:17]))
            step(dve, V.tensor_copy(cw[:, :, E:UNITS], ex[:, :, 16:17].to_broadcast([P, B, 4])))
            for k in range(B * UNITS):
                u, b = k // B, k % B
                dve.wait_ge(sem("g_gated"), k + 1)
                V.scalar_tensor_tensor(H[:, b, u * EI:(u + 1) * EI], ps[:, 2 + k % 4, EI:2 * EI], cw[:, b, u:u + 1],
                                       esg[:, k % 4], ALU.mult, ALU.mult).then_inc(sem("h_ready"), 1)
            dve.wait_ge(sem("downed"), DT // 2)
            add_output(dve, [ps[:, 0, 0:D], ps[:, 1, 0:D]], True)

        def tensor_rest(pe):
            for n, part in enumerate((tensor_attention, tensor_ffn, None, tensor_phase, tensor_experts)):
                if part and stop > n:
                    part(pe)

        def scalar_rest(act):
            def summary(act):
                nc.scalar.preload_act_table_set("natural_log_exp_and_others")
                ln_rstd(act, LN_OF["summary"])
                ln_rstd(act, LN_OF["summary2"])
            for n, part in enumerate((scalar_attention, scalar_ffn, summary, scalar_phase, scalar_experts)):
                if stop > n:
                    part(act)

        def vector_rest(dve):
            for n, part in enumerate((vector_attention, vector_ffn, vector_summary, vector_phase, vector_experts)):
                if stop > n:
                    part(dve)

        def pool_rest(pool):
            G = nc.gpsimd
            pool.wait_ge(sem("w_phase"), loaded["w_phase"])
            pool.wait_ge(sem("w_ri_loaded"), 16)
            for c in range(2):
                G.tensor_tensor(w_ri[:, c], w_ri[:, c], w_nrm[:, :, None].to_broadcast([P, FT, 96]), ALU.mult
                                ).then_inc(sem("w_ri_ready"), 1)
            pool.wait_ge(sem("attn_out"), 1)
            for kt in range(KT):
                G.tensor_tensor(w_cm[:, kt], w_mem[:, kt, None, :].to_broadcast([P, CONV, 288]), w_conv[:], ALU.mult
                                ).then_inc(sem("w_cm_ready"), 1)
            if stop >= 4:
                pool_phase(pool)
            if stop >= 5:
                pool_experts(pool)
        @block.vector
        def _(dve):
            V = nc.vector
            V.memset(ones[:], 1.0).then_inc(sem("ones_set"), 1)
            V.memset(zer, 0.0).then_inc(sem("zeros_set"), 1)
            V.memset(xnT[:, :, :, 0:3], 0.0)
            V.memset(v_sb[:, :, :, 8:9], 1.0)
            step(dve, V.memset(qbd, 0.0))
            dve.wait_ge(sem("x_loaded"), 32)
            ln_stats(dve, 0)
            ln_copy(dve, 0, 0)
            dve.wait_ge(sem("w_x"), 32)
            step(dve, V.tensor_copy(wkv_half[:, 0], w_xkv))
            V.tensor_tensor(wkv_half[:, 1], w_xkv, wkv_half[:, 0].bitcast(F32), ALU.subtract).then_inc(sem("wkv_split"), 1)
            dve.wait_ge(sem("q_projected"), 1)
            V.tensor_copy(qraw, ps[:, 1].rearrange("p (b n) -> p b n", b=B)).then_inc(sem("q_copied"), 1)
            dve.wait_ge(sem("q_squared"), 1)
            V.tensor_reduce(qms[:], qsq.rearrange("p b (h d) -> p b h d", d=XD), AX_X, ALU.add
                            ).then_inc(sem("q_meansq"), 1)
            dve.wait_ge(sem("q_rstd"), 1)
            for b in range(B):
                qn = xn[:, b]
                step(dve, V.tensor_tensor(qn.rearrange("p (h d) -> p h d", d=XD),
                                          qraw[:, b].rearrange("p (h d) -> p h d", d=XD),
                                          qrs[:, b, :, None].to_broadcast([P, XH, XD]), ALU.mult))
                pack = qpack[:, b].rearrange("p (h s r d) -> p h s r d", s=2, r=2, d=XD)
                qn2 = qn.rearrange("p (h d) -> p h d", d=XD)[:, :, None, :].to_broadcast([P, XH, 2, XD])
                step(dve, V.tensor_copy(pack[:, :, 0], qn2))
                V.tensor_tensor(pack[:, :, 1], qn2, pack[:, :, 0], ALU.subtract).then_inc(sem("q_packed"), 1)

            def take_q(b, bank):
                dve.wait_ge(sem("q_transposed"), b + 1)
                t = ps[:, bank].bitcast(F16).rearrange("p (g n) -> p g n", g=GROUPS)
                for j in range(4):
                    rows = slice(32 * j, 32 * j + 32)
                    i = V.tensor_copy(qbd[rows, b, :, (j % 2) * P:(j % 2 + 1) * P], t[rows])
                i.then_inc(sem("q_ready"), 1)

            def take_kv(t, s):
                dve.wait_ge(sem("kv_projected"), t + 1)
                V.tensor_copy(kraw[:, s % 2], ps[:, 6, 0:256]).then_inc(sem("k_taken"), 1)
                if not (isinstance(t, int) and t < V_SLOTS):
                    dve.wait_ge(sem("pv_done"), 4 * t - 12)
                V.tensor_copy(v_sb[:, s, :, 0:8], ps[:, 6, 256:512].rearrange("p (h d) -> p h d", d=XD)
                              ).then_inc(sem("kv_taken"), 1)

            def mean_squares(t, s):
                dve.wait_ge(sem("k_squared"), t + 1)
                V.tensor_reduce(kms[:, s % 2], ksq[:, s % 2].rearrange("p (h d) -> p h d", d=XD), AX_X, ALU.add
                                ).then_inc(sem("k_meansq"), 1)

            def pack_keys(t, s):
                dve.wait_ge(sem("k_rstd"), t + 1)
                knb = kn.rearrange("p (h d) -> p h d", d=XD)
                V.tensor_tensor(knb, kraw[:, s % 2].rearrange("p (h d) -> p h d", d=XD),
                                krs[:, s % 2, :, None].to_broadcast([P, XH, XD]), ALU.mult
                                ).then_inc(sem("k_normed"), 1)
                if not (isinstance(t, int) and t < 2):
                    dve.wait_ge(sem("k_transposed"), t - 1)
                dve.wait_ge(sem("k_normed"), t + 1)
                pack = kpack[:, s % 2].rearrange("p (h s r d) -> p h s r d", s=2, r=2, d=XD)
                kn2 = knb[:, :, None, :].to_broadcast([P, XH, 2, XD])
                V.tensor_copy(pack[:, :, :, 0], kn2).then_inc(sem("k_high"), 1)
                dve.wait_ge(sem("k_high"), t + 1)
                V.tensor_tensor(pack[:, :, :, 1], kn2, pack[:, :, :, 0], ALU.subtract
                                ).then_inc(sem("k_packed"), 1)

            def take_keys(t, s):
                dve.wait_ge(sem("k_transposed"), t + 1)
                if not (isinstance(t, int) and t < 2):
                    dve.wait_ge(sem("scores_done"), 4 * t - 4)
                V.tensor_copy(kT[:, s % 2], ps[:, 7].bitcast(F16).rearrange("p (g m) -> p g m", g=GROUPS)
                              ).then_inc(sem("k_ready"), 1)

            def kv_step(t, s, first=False):
                if not (isinstance(t, int) and t >= NB):
                    take_kv(t, s)
                if not (isinstance(t, int) and t < 2):
                    take_keys(t - 2, (s - 2) % 4)
                if not (isinstance(t, int) and not 1 <= t <= NB):
                    pack_keys(t - 1, (s - 1) % 4)
                if not (isinstance(t, int) and t >= NB):
                    mean_squares(t, s)

            def take_acc(b):
                dve.wait_ge(sem("acc_done"), b + 1)
                V.tensor_copy(accs[:, b], ps[:, 4:6].rearrange("p c n -> p (c n)")).then_inc(sem("acc_taken"), 1)

            take_kv(0, 0)
            take_q(0, 3)
            mean_squares(0, 0)
            kv_step(1, 1)
            dve.wait_ge(sem("decay_exp"), 1)
            step(dve, V.tensor_scalar(dec[:, 1:2], dec[:, 0:1], 1.0, None, ALU.add))
            step(dve, V.reciprocal(dec[:, 2:3], dec[:, 1:2]))
            V.tensor_tensor_scan(geo, dec[:, 2:3].to_broadcast([P, M]), ones[:, 0:1].to_broadcast([P, M]),
                                 0.0, ALU.mult, ALU.add).then_inc(sem("geo_ready"), 1)

            for t in range(2, 4):
                kv_step(t, t)
            take_q(1, 7)
            with dve.Fori(1, MB // 4) as q:
                for s in range(4):
                    kv_step(4 * q + s, s)
            for s in range(4):
                if s == 3:
                    take_acc(0)
                kv_step(MB + s, s)
            with dve.Fori(MB // 4 + 1, NB // 4) as q:
                for s in range(4):
                    kv_step(4 * q + s, s)
            kv_step(NB, 0)
            kv_step(NB + 1, 1)
            take_acc(1)
            dve.wait_ge(sem("ctx_weighted"), NB)
            step(dve, V.tensor_reduce(usum[:].rearrange("p k b -> p b k"), uacc, AX_X, ALU.add))
            step(dve, V.tensor_reduce(gsum[:], geo, AX_X, ALU.add))
            dve.wait_ge(sem("w_sum"), loaded["w_sum"])
            V.tensor_scalar(bg[:], b_in[:], gsum[:, 0:1], None, ALU.mult).then_inc(sem("u_ready"), 1)
            for b in range(B):
                dve.wait_ge(sem("acc_transposed"), b + 1)
                t = ps[:, 2 * b:2 * b + 2].rearrange("p c (h r) -> p (c h) r", r=32)
                step(dve, V.reciprocal(rden[:, b, :, None], t[:, :, 8:9]))
                step(dve, V.tensor_tensor(xn[:, b].rearrange("p (h d) -> p h d", d=XD), t[:, :, 0:8],
                                          rden[:, b, :, None].to_broadcast([P, XH, XD]), ALU.mult))
                i = V.tensor_tensor(x[:, b], x[:, b], xn[:, b], ALU.add)
                if stop == 0:
                    i.then_inc(sem("x_final"), 1)
                else:
                    step(dve, i)
            if stop == 0:
                return
            vector_rest(dve)

        @block.gpsimd
        def _(pool):
            G = nc.gpsimd
            G.memset(uacc, 0.0).then_inc(sem("uacc_zero"), 1)
            pool.wait_ge(sem("uacc_zero"), 1)

            def square_keys(t, s):
                pool.wait_ge(sem("k_taken"), t + 1)
                G.tensor_tensor(ksq[:, s % 2], kraw[:, s % 2], kraw[:, s % 2], ALU.mult).then_inc(sem("k_squared"), 1)

            def split_low(t, s):
                pool.wait_ge(sem("ctx_high"), t + 1)
                G.tensor_tensor(ctx_half[:, s % 2, 1], ctxT[:, s], ctx_half[:, s % 2, 0].bitcast(F32), ALU.subtract
                                ).then_inc(sem("ctx_split"), 1)

            def weigh_context(t, s, b, q4):
                pool.wait_ge(sem(f"ctx_loaded{s}"), 16 * (q4 + 1))
                if isinstance(t, int):
                    pool.wait_ge(sem("geo_ready"), 1)
                g = geo[:, None, bass.ds((t - MB * b) * P, P)].to_broadcast([P, KT, P])
                G.tensor_tensor(gprod[:, s % 2], ctxT[:, s], g, ALU.mult).then_inc(sem("ctx_weighed"), 1)
                pool.wait_ge(sem("ctx_weighed"), t + 1)
                G.tensor_tensor(uacc[:, b], uacc[:, b], gprod[:, s % 2], ALU.add).then_inc(sem("ctx_weighted"), 1)

            for t in range(3):
                split_low(t, t)
            for t in range(2):
                square_keys(t, t)
            split_low(3, 3)
            for t in range(4):
                weigh_context(t, t, 0, 0)
            for b in range(B):
                with pool.Fori(b * (MB // 4 - 1), (b + 1) * MB // 4 - 1) as q:
                    for s in range(4):
                        square_keys(4 * q + (s + 2), s)
                        split_low(4 * q + (s + 4), s)
                        weigh_context(4 * q + (s + 4), s, b, q + 1)
            for t in range(NB - 2, NB):
                square_keys(t, t)
            if stop >= 1:
                pool_rest(pool)

        @block.scalar
        def _(act):
            nc.scalar.preload_act_table_set("natural_log_exp_and_others")
            ln_rstd(act, 0)
            act.wait_ge(sem("q_copied"), 1)
            nc.scalar.activation(qsq, qraw, ACT.Square).then_inc(sem("q_squared"), 1)
            act.wait_ge(sem("q_meansq"), 1)
            nc.scalar.activation(qrs[:], qms[:], ACT.Ln, bias=1e-6, scale=1.0 / XD).then_inc(sem("q_log"), 1)
            act.wait_ge(sem("q_log"), 1)
            nc.scalar.activation(qrs[:], qrs[:], ACT.Exp, scale=-0.5).then_inc(sem("q_rstd"), 1)

            act.wait_ge(sem("decay_loaded"), 16)
            nc.scalar.activation(dec[:, 0:1], decay[:], ACT.Exp, scale=-1.0).then_inc(sem("decay_exp"), 1)

            def split_high(t, s, q4):
                act.wait_ge(sem(f"ctx_loaded{s}"), 16 * (q4 + 1))
                if not (isinstance(t, int) and t < 2):
                    act.wait_ge(sem("kv_projected"), t - 1)
                nc.scalar.copy(ctx_half[:, s % 2, 0], ctxT[:, s]).then_inc(sem("ctx_high"), 1)

            for t in range(4):
                split_high(t, t, 0)

            def key_rstd(t, s):
                act.wait_ge(sem("k_meansq"), t + 1)
                nc.scalar.activation(kln, kms[:, s % 2], ACT.Ln, bias=1e-6, scale=1.0 / XD).then_inc(sem("k_log"), 1)
                act.wait_ge(sem("k_log"), t + 1)
                nc.scalar.activation(krs[:, s % 2], kln, ACT.Exp, scale=-0.5).then_inc(sem("k_rstd"), 1)

            def exps(t, s, r):
                act.wait_ge(sem("scores_done"), 4 * t + r + 1)
                if not (isinstance(t, int) and t < 1):
                    act.wait_ge(sem("pv_done"), 4 * t + r - 3)
                nc.scalar.activation(probs[:, r].rearrange("p a g j n -> p a (g j n)"), ps[:, 2 * (r % 2):2 * (r % 2) + 2],
                                     ACT.Exp, scale=XD ** -0.5).then_inc(sem("exp_done"), 1)

            key_rstd(0, 0)
            key_rstd(1, 1)

            def act_step(t, s, q4):
                for r in range(ROUNDS):
                    exps(t, s, r)
                    if r == 0 and not (isinstance(t, int) and t + 2 >= NB):
                        key_rstd(t + 2, (s + 2) % 4)
                    if r == 0 and not (isinstance(t, int) and t + 4 >= NB):
                        split_high(t + 4, s, q4 + 1)

            for t in range(4):
                act_step(t, t, 0)
                share = -(-len(loads) // 4)
                for name, dst, src in loads[share * t:share * (t + 1)]:
                    act.dma_start(dst, src).then_inc(sem(name), 16)
            with act.Fori(1, NB // 4 - 1) as q:
                for s in range(4):
                    act_step(4 * q + s, s, q)
            for t in range(NB - 4, NB):
                act_step(t, t % 4, NB // 4 - 1)
            if stop >= 1:
                scalar_rest(act)

        @block.tensor
        def _(pe):
            T = nc.tensor
            def project(t, s):
                pe.wait_ge(sem("ctx_split"), t + 1)
                if not (isinstance(t, int) and t < 1):
                    pe.wait_ge(sem("kv_taken"), t)
                for n, (c, d) in enumerate(HALF_PRODUCTS):
                    for kt in range(KT):
                        i = T.matmul(ps[:, 6], ctx_half[:, s % 2, c, kt], wkv_half[:, d, kt], start=(n + kt == 0),
                                     stop=(n == 2 and kt == KT - 1))
                i.then_inc(sem("kv_projected"), 1)

            pe.wait_ge(sem("w_x"), 32)
            pe.wait_ge(sem("x_loaded"), 32)
            ln_transpose(pe, 0, 0)
            pe.wait_ge(sem("xnT_ready"), 1)
            pe.wait_ge(sem("wq_loaded"), 16)
            for b in range(B):
                for kt in range(KT):
                    i = T.matmul(ps[:, 1, b * 256:b * 256 + 256], xnT[:, kt, b, 3:], w_xq[:, kt],
                                 start=(kt == 0), stop=(kt == KT - 1))
            i.then_inc(sem("q_projected"), 1)
            pe.wait_ge(sem("wkv_split"), 1)
            project(0, 0)
            pe.wait_ge(sem("zeros_set"), 1)

            def turn_keys(t, s):
                pe.wait_ge(sem("k_packed"), t + 1)
                if isinstance(t, int) and t == 2:
                    pe.wait_ge(sem("q_ready"), 2)
                if not (isinstance(t, int) and t < 1):
                    pe.wait_ge(sem("k_ready"), t)
                out = ps[:, 7].bitcast(F16)
                for g in range(GROUPS):
                    i = T.transpose(out[:, g * P:(g + 1) * P], kpack[:, s % 2, g * P:(g + 1) * P], id16[:])
                i.then_inc(sem("k_transposed"), 1)

            def scores(b, t, s, r):
                if not (isinstance(t, int) and 4 * t + r < 2):
                    pe.wait_ge(sem("exp_done"), 4 * t + r - 1)
                for gg in range(2):
                    g = 2 * r + gg
                    for a in range(2):
                        rows = slice(64 * a, 64 * a + 64)
                        i = T.matmul(ps[:, 2 * (r % 2) + a, gg * 256:gg * 256 + 256], kT[rows, s % 2, g],
                                     qbd[rows, b, g], start=True, stop=True)
                i.then_inc(sem("scores_done"), 1)

            def values(s, r):
                for gg in range(2):
                    g = 2 * r + gg
                    for j in range(4):
                        i = T.matmul(ps[32 * j:32 * j + 9, 4 + g // 4, (g % 4) * P:(g % 4 + 1) * P],
                                     v_sb[:, s, 4 * g + j], probs[:, r, j // 2, gg, j % 2],
                                     start=False, stop=False, skip_group_check=True)
                i.then_inc(sem("pv_done"), 1)

            def open_acc():
                for c in range(2):
                    T.matmul(ps[:, 4 + c], zer[:, 0:128], zer, start=True, stop=False, skip_group_check=True)

            def pe_step(b, t, s, q4, lag=True):
                tt = t if isinstance(t, int) else None
                for r in range(ROUNDS):
                    if r == 0:
                        pe.wait_ge(sem("k_ready"), t + 1)
                    scores(b, t, s, r)
                    if tt == 0 and r < 2:
                        pass
                    else:
                        if tt == MB and r == 2:
                            pe.wait_ge(sem("acc_taken"), 1)
                            open_acc()
                        if r < 2:
                            values((s - 1) % 4, r + 2)
                        else:
                            values(s, r - 2)
                        if tt == MB and r == 1:
                            T.matmul(ps[:, 4, 0:1], zer[:, 0:128], zer[:, 0:1], start=False, stop=False,
                                     skip_group_check=True).then_inc(sem("acc_done"), 1)
                    if r == 0 and not (tt is not None and tt + 3 >= NB):
                        s3 = (s + 3) % 4
                        project(t + 3, s3)
                    if r == 1 and not (tt is not None and tt + 1 >= NB):
                        turn_keys(t + 1, (s + 1) % 4)

            def turn_queries(b, bank):
                pe.wait_ge(sem("q_packed"), b + 1)
                for g in range(GROUPS):
                    i = T.transpose(ps[:, bank].bitcast(F16)[:, g * P:(g + 1) * P], qpack[:, b, g * P:(g + 1) * P], id16[:])
                i.then_inc(sem("q_transposed"), 1)

            turn_queries(0, 3)
            open_acc()
            for t in range(1, 3):
                project(t, t)
            turn_keys(0, 0)
            pe.wait_ge(sem("q_ready"), 1)
            for t in range(4):
                pe_step(0, t, t, 0)
                if t == 0:
                    pe.wait_ge(sem("k_ready"), 2)
                    turn_queries(1, 7)
            with pe.Fori(1, MB // 4) as q:
                for s in range(4):
                    pe_step(0, 4 * q + s, s, q)
            for s in range(4):
                pe_step(1, MB + s, s, MB // 4)
            with pe.Fori(MB // 4 + 1, NB // 4 - 1) as q:
                for s in range(4):
                    pe_step(1, 4 * q + s, s, q)
            for s in range(4):
                pe_step(1, NB - 4 + s, s, NB // 4 - 1)
            for r in range(2, 4):
                pe.wait_ge(sem("exp_done"), 4 * NB - 3 + r)
                values(3, r)
            T.matmul(ps[:, 4, 0:1], zer[:, 0:128], zer[:, 0:1], start=False, stop=False,
                     skip_group_check=True).then_inc(sem("acc_done"), 1)
            for b in range(B):
                pe.wait_ge(sem("acc_taken"), b + 1)
                for g in range(GROUPS):
                    i = T.transpose(ps[:, 2 * b + g // 4, (g % 4) * P:(g % 4 + 1) * P], accs[:, b, g * P:(g + 1) * P],
                                    id32[:])
                i.then_inc(sem("acc_transposed"), 1)
            if stop >= 1:
                tensor_rest(pe)


def layout(inputs):
    import numpy as np

    f = {k: np.asarray(v) for k, v in inputs.items()}
    A = {}

    def tiles(a):
        return a.reshape(-1, P, a.shape[-1]).transpose(1, 0, 2)

    def rows(a):
        return np.broadcast_to(a.reshape(1, -1), (P, a.size))

    def padded(a, n):
        return np.concatenate([a, np.zeros((n - a.shape[0],) + a.shape[1:], a.dtype)])

    A["x"] = f["x"]
    c = f["ctx_2048"][:, ::-1].reshape(B, MB, P, KT, P)
    A["ctx"] = c.transpose(0, 1, 4, 3, 2).reshape(NB, P, KT, P)
    A["w_xq"] = tiles(f["L0_xattn_Wq"].T)
    kv = np.concatenate([f["L0_xattn_Wk"], f["L0_xattn_Wv"]])
    A["w_xkv"] = tiles(np.concatenate([kv[0::2], kv[1::2]]).T)
    for n in "qkv":
        A[f"w_{n}"] = tiles(f[f"L0_attn_w_{n}"])
    A["w_o"] = tiles(f["L0_attn_w_o"])
    A["b_qkv"] = np.stack([f[f"L0_attn_b_{n}"].reshape(AH, AD).T for n in "qkv"], 1)
    A["b_o"] = rows(f["L0_attn_b_o"])
    w1, w3 = (tiles(padded(f[f"L0_ffn_{n}"], HT_FFN * P).T).reshape(P, -1) for n in ("w1", "w3"))
    w2 = tiles(padded(f["L0_ffn_w2"].T, HT_FFN * P)).reshape(P, -1)
    A["w_ffn"] = np.stack([w1, w3, w2], 1)
    A["decay"] = rows(f["L1_xattn_decay"].reshape(1))
    A["w_in"] = tiles(f["L1_xattn_W_in"].T)
    A["w_out1"] = tiles(f["L1_xattn_W_out"].T)
    A["b_in"] = f["L1_xattn_b_in"].reshape(KT, P).T
    A["vecs"] = np.stack([rows(f[f"L1_xattn_{n}"]) for n in ("b_out", "gamma", "beta")], 1)
    A["w_mem"] = tiles(f["L1_attn_W_mem"])
    A["w_conv"] = np.broadcast_to(f["L1_attn_conv_k"].reshape(1, CONV, 288), (P, CONV, 288))
    q = f["L1_attn_W_q"].reshape(D, 4, CH * CM, 2).transpose(0, 1, 3, 2)
    A["w_q4"] = tiles(np.concatenate([q, q], 3).reshape(D, 1024))
    A["theta"] = rows(f["L1_attn_theta"])
    w = np.zeros((2, FT, 2, CH, CM, 2, SW), np.float32)
    for c, n in enumerate(("W_re", "W_im")):
        a = f[f"L1_attn_{n}"].reshape(FT, 2, CH, 1, SW)
        for k in range(2):
            w[c, :, k, :, :, k] = a[:, k]
    A["w_ri"] = w.reshape(2, FT, P, 96).transpose(2, 0, 1, 3)
    A["w_nrm"] = np.broadcast_to(f["L1_attn_norm_scale"].reshape(FT, 2 * CH, 1), (FT, 2 * CH, CM)).reshape(FT, P).T
    l = np.arange(P, dtype=np.float32)[:, None]
    dist = np.concatenate([np.broadcast_to(l - (L - 1), (P, 28)), np.broadcast_to(-l, (P, 4))], 1)
    slopes = np.concatenate([f["L1_attn_decay_slopes"], f["L1_attn_anchor_slopes"]])
    A["small"] = np.stack([rows(slopes), rows(f["L1_attn_score_scale"]), dist], 1)
    A["w_out2"] = tiles(f["L1_attn_W_out"])
    A["w_rt"] = tiles(np.concatenate([f["L1_ffn_gate_w"], f["L1_ffn_shared_gate_vec"]]).T)
    shared = f["L1_ffn_shared_gate_up"].reshape(2, 4, EI, D).transpose(1, 0, 2, 3).reshape(4, 2 * EI, D)
    gu = np.concatenate([f["L1_ffn_expert_gate_up"], shared]).reshape(UNITS * 2 * EI, D)
    A["w_gu"] = gu.T.reshape(KT, P, UNITS * 2 * EI)
    down = np.concatenate([f["L1_ffn_expert_down"].transpose(0, 2, 1).reshape(E * EI, D), f["L1_ffn_shared_down"].T])
    A["w_down"] = tiles(padded(down, DT * P))
    A["id32"] = np.eye(P, dtype=np.float32)
    A["id16"] = np.eye(P, dtype=np.float16)
    A["tri"] = np.triu(np.ones((P, P), np.float32))
    A["mask"] = np.where(np.tril(np.ones((P, P))) > 0, 0.0, -1e10).astype(np.float32)
    A["iota"] = rows(np.arange(E, dtype=np.float32))
    return {k: np.ascontiguousarray(v) for k, v in A.items()}


def kernel(**inputs):
    import concourse.bacc as bacc
    from concourse.bass_utils import run_bass_kernel_spmd

    nc = bacc.Bacc("TRN2", target_bir_lowering=False, num_devices=1)
    io, arrays = {}, {}
    for name, a in layout(inputs).items():
        arrays[f"in_{name}"] = a
        io[name] = nc.dram_tensor(f"in_{name}", a.shape, mybir.dt.from_np(a.dtype), kind="ExternalInput").ap()
    io["out"] = nc.dram_tensor("out", (B, L, D), F32, kind="ExternalOutput").ap()
    build_program(nc, io)
    return run_bass_kernel_spmd(nc, [arrays], core_ids=[0]).results[0]["out"]
```

```python
from contextlib import ExitStack
import math

import concourse.bass as bass
from concourse import mybir

F32 = mybir.dt.float32
F16 = mybir.dt.float16
F32R = mybir.dt.float32r
U32 = mybir.dt.uint32
ALU = mybir.AluOpType
ACT = mybir.ActivationFunctionType
AX_X = mybir.AxisListType.X

P = 128
B, L, D = 2, 128, 256
KT = D // P
M = 2048
MB = M // P
NB = B * MB
XH, XD = 32, 8
GROUPS = XH // 4
ROUNDS = GROUPS // 2
CTX_SLOTS = V_SLOTS = P_SLOTS = 4
AH, AD = 16, 128
HID, HT_FFN = 682, 6
FCHUNK = HT_FFN * D // 4
CK, CH, CM = 32, 8, 8
NF = CK * CH * CM
FT = NF // P
CONV = 4
SW = 48
E, TOPK, EI = 16, 4, 176
UNITS = E + 4
DT = 28
TWO_PI = 2.0 * math.pi
ARENA = 10048
ROUND_MAGIC = 1.5 * 2.0 ** 23


def build_program(nc, io):
    ctx = ExitStack()
    with ctx:
        sems = {}

        def sem(name):
            if name not in sems:
                sems[name] = ctx.enter_context(nc.semaphore(name))
            return sems[name]

        def sb(name, shape, dt=F32):
            return ctx.enter_context(nc.sbuf_tensor("sb_" + name, shape, dt))

        ps = ctx.enter_context(nc.psum_tensor("ps", [P, 8, 512], F32))
        x = sb("x", [P, B, D])
        xn = sb("xn", [P, B, D])
        xnT = sb("xnT", [P, KT, B, 3 + L])
        bn = sb("bn", [P, B, 6])
        mv = sb("mv", [P, B, 2])
        lnv = sb("lnv", [P, B])
        rstd = sb("rstd", [P, B])
        id32 = sb("id32", [P, P])
        id16 = sb("id16", [P, P], F16)
        ones = sb("ones", [P, P])
        tri = sb("tri", [P, P])
        mask = sb("mask", [P, L])

        w_x = sb("w_x", [P, 3 * KT * D])
        w_xq = w_x[:, 0:KT * D].rearrange("p (k n) -> p k n", k=KT)
        w_xkv = w_x[:, KT * D:].rearrange("p (k n) -> p k n", k=KT)
        w_out2 = w_x[:].rearrange("p (t n) -> p t n", t=6)
        big = sb("big", [P, 3 * KT * 2048 + 1792])
        w_qkv = big[:, 0:3 * KT * 2048].rearrange("p (s k n) -> p s k n", s=3, k=KT)
        w_gu = big[:, 0:KT * UNITS * 2 * EI].rearrange("p (k n) -> p k n", k=KT)
        mid = sb("mid", [P, AH * D + 3 * HT_FFN * D])
        w_o = mid[:, 0:AH * D].rearrange("p (h n) -> p h n", h=AH)
        w_ffn = mid[:, AH * D:].rearrange("p (w n) -> p w n", w=3)
        w_cm = mid[:, 0:KT * CONV * 288].rearrange("p (k w n) -> p k w n", k=KT, w=CONV)
        w_down = mid[:, 0:DT * D].rearrange("p (t n) -> p t n", t=DT)
        b_qkv = sb("b_qkv", [P, 3, AH])
        b_o = sb("b_o", [P, D])
        w_in = sb("w_in", [P, KT, D])
        w_out1 = sb("w_out1", [P, KT, D])
        b_in = sb("b_in", [P, KT])
        vecs = sb("vecs", [P, 3, D])
        decay = sb("decay", [P, 1])
        w_mem = sb("w_mem", [P, KT, 288])
        w_conv = sb("w_conv", [P, CONV, 288])
        w_q4 = sb("w_q4", [P, KT, 1024])
        w_ri = sb("w_ri", [P, 2, FT, 96])
        w_nrm = sb("w_nrm", [P, FT])
        small = sb("small", [P, 4, 32])
        w_rt = sb("w_rt", [P, KT, 17])
        iota = sb("iota", [P, E])

        theta = sb("theta", [P, NF])
        geo = w_q4[:].rearrange("p k n -> p (k n)")
        accs = theta[:].rearrange("p (b n) -> p b n", b=B)

        qraw = accs[:, 1, 0:512].rearrange("p (b n) -> p b n", b=B)
        qpack = accs[:, 0].bitcast(F16).rearrange("p (b n) -> p b n", b=B)
        qsq = accs[:, 1, 512:1024].rearrange("p (b n) -> p b n", b=B)
        qms = sb("qms", [P, B, XH])
        qrs = sb("qrs", [P, B, XH])

        arena = sb("arena", [P, ARENA])

        def cut(start, n):
            return arena[:, start:start + n]

        halves = sb("halves", [P, 3840], F32R)
        wkv_half = halves[:, 0:2048].rearrange("p (c k n) -> p c k n", c=2, k=KT)
        ctx_half = halves[:, 2048:3072].rearrange("p (s c k m) -> p s c k m", s=2, c=2, k=KT)
        HALF_PRODUCTS = ((0, 0), (1, 0), (0, 1))

        o = 0
        ctxT = cut(o, 4 * 256).rearrange("p (s k m) -> p s k m", s=4, k=KT); o += 1024
        kraw = cut(o, 512).rearrange("p (s n) -> p s n", s=2); o += 512
        kms = cut(o, 64).rearrange("p (s n) -> p s n", s=2); o += 64
        krs = cut(o, 64).rearrange("p (s n) -> p s n", s=2); o += 64
        kln = cut(o, 32); o += 32
        kn = cut(o, 256); o += 256
        kpack = cut(o, 1024).bitcast(F16).rearrange("p (s n) -> p s n", s=2); o += 1024
        kT = cut(o, 1024).bitcast(F16).rearrange("p (s g m) -> p s g m", s=2, g=GROUPS); o += 1024
        v_sb = cut(o, 4 * 288).rearrange("p (s h c) -> p s h c", s=4, h=XH); o += 1152
        probs = cut(o, 4096).rearrange("p (s a g j n) -> p s a g j n", s=4, a=2, g=2, j=2); o += 4096
        ksq = big[:, 12288:12800].rearrange("p (s n) -> p s n", s=2)
        gprod = big[:, 12800:13312].rearrange("p (s k m) -> p s k m", s=2, k=KT)
        uacc = big[:, 13312:13824].rearrange("p (b k m) -> p b k m", b=B, k=KT)
        qbd = w_ri[:].rearrange("p c t n -> p (c t n)")[:, 0:2048].bitcast(F16).rearrange(
            "p (b g n) -> p b g n", b=B, g=GROUPS)
        zer = cut(o, 256).bitcast(F16); o += 256
        rden = cut(o, 64).rearrange("p (b h) -> p b h", b=B); o += 64
        tern = cut(o, FCHUNK); o += FCHUNK
        fsc = cut(o, 16); o += 16
        w_tern = mid[:, AH * D:AH * D + 3 * HT_FFN * D // 2].bitcast(F16).rearrange("p (w n) -> p w n", w=3)
        assert o <= ARENA, o
        dec = sb("dec", [P, 4])
        usum = sb("usum", [P, KT, B])
        gsum = sb("gsum", [P, 1])
        smean = sb("smean", [P, KT, B])
        bg = sb("bg", [P, KT])
        pw = sb("pw", [P, B, 32])
        logw = sb("logw", [P, 6, 32])
        iden = sb("iden", [P, B, 32])

        loads = [
            ("w_attn", w_qkv[:, 0], io["w_q"]), ("w_attn", w_qkv[:, 1], io["w_k"]),
            ("w_attn", w_qkv[:, 2], io["w_v"]), ("w_attn", w_o, io["w_o"]),
            ("w_attn", b_qkv[:], io["b_qkv"]), ("w_attn", b_o[:], io["b_o"]),
            ("w_attn", mask[:], io["mask"]),
            ("w_ffn", w_ffn, io["w_ffn"]),
            ("w_sum", w_in[:], io["w_in"]), ("w_sum", w_out1[:], io["w_out1"]),
            ("w_sum", b_in[:], io["b_in"]), ("w_sum", vecs[:], io["vecs"]),
            ("w_phase", w_mem[:], io["w_mem"]), ("w_phase", w_conv[:], io["w_conv"]),
            ("w_phase", w_nrm[:], io["w_nrm"]), ("w_phase", small[:, 0:3], io["small"]),
            ("w_phase", tri[:], io["tri"]),
            ("w_moe", w_rt[:], io["w_rt"]), ("w_moe", iota[:], io["iota"]),
        ]
        loaded = {}
        for name, _, _ in loads:
            loaded[name] = loaded.get(name, 0) + 16
        block = ctx.enter_context(nc.Block())

        LN_OF = {"xattn": 0, "attn": 1, "ffn": 2, "summary": 3, "summary2": 4, "phase": 5, "moe": 6}
        WARM = {0: 20, 1: 24, 2: 28, 5: 75, 6: 24}

        @block.sync
        def _(sp):
            sp.dma_start(x[:], io["x"].rearrange("b l d -> l b d")).then_inc(sem("x_loaded"), 16)
            sp.dma_start(id32[:], io["id32"]).then_inc(sem("x_loaded"), 16)
            sp.dma_start(decay[:], io["decay"]).then_inc(sem("decay_loaded"), 16)
            sp.dma_start(w_xq, io["w_xq"]).then_inc(sem("wq_loaded"), 16)
            sp.dma_start(w_xkv, io["w_xkv"]).then_inc(sem("wkv_loaded"), 16)
            for s in range(CTX_SLOTS):
                sp.dma_start(ctxT[:, s], io["ctx"][s]).then_inc(sem(f"ctx_loaded{s}"), 16)
                if s == 0:
                    sp.dma_start(id16[:], io["id16"]).then_inc(sem("id16_loaded"), 16)
            with sp.Fori(1, NB // 4) as q:
                for s in range(CTX_SLOTS):
                    sp.wait_ge(sem("ctx_split"), 4 * q + (s - 3))
                    sp.wait_ge(sem("ctx_weighted"), 4 * q + (s - 3))
                    sp.dma_start(ctxT[:, s], io["ctx"][bass.ds(4 * q + s, 1)].rearrange("o p k m -> p (o k) m")
                                 ).then_inc(sem(f"ctx_loaded{s}"), 16)
            sp.wait_ge(sem("ctx_weighted"), NB)
            sp.wait_ge(sem("u_ready"), 1)
            sp.dma_start(w_ri[:], io["w_ri"]).then_inc(sem("w_ri_loaded"), 16)
            sp.dma_start(w_out2, io["w_out2"]).then_inc(sem("late_loaded"), 16)
            sp.dma_start(w_q4[:], io["w_q4"]).then_inc(sem("late_loaded"), 16)
            sp.wait_ge(sem("acc_transposed"), 2 * B)
            sp.dma_start(theta[:], io["theta"]).then_inc(sem("late_loaded"), 16)
            sp.wait_ge(sem("qk_projected"), AH)
            sp.wait_ge(sem("v_projected"), 2 * AH // 4)
            for k in range(KT):
                sp.dma_start(w_gu[:, k], io["w_gu"][k]).then_inc(sem("gu_loaded"), 16)
            sp.wait_ge(sem("y_gated"), 3 * B)
            sp.wait_ge(sem("last_y_gated"), B)
            sp.dma_start(w_down, io["w_down"]).then_inc(sem("down_loaded"), 16)
            sp.wait_ge(sem("x_final"), B)
            sp.dma_start(io["out"].rearrange("b l d -> l b d"), x[:]).then_inc(sem("stored"), 16)
            sp.wait_ge(sem("stored"), 16)

        xa_half = halves[:, 0:1024].rearrange("p (c k n) -> p c k n", c=2, k=KT)
        qk_half = halves[:, 1024:3072].rearrange("p (s c w k n) -> p s c w k n", s=2, c=2, w=2, k=KT)
        qT = cut(0, 512).rearrange("p (s n) -> p s n", s=2)
        kT2 = cut(512, 512).rearrange("p (s n) -> p s n", s=2)
        v_at = cut(1024, 2 * 2 * 512).rearrange("p (s b n) -> p s b n", s=2, b=B)
        s_at = cut(3072, 512).rearrange("p (s b n) -> p s b n", s=2, b=B)
        p_at = cut(3584, 512).rearrange("p (s b n) -> p s b n", s=2, b=B)
        pT_at = cut(4096, 512).rearrange("p (s b n) -> p s b n", s=2, b=B)
        oT_at = cut(4608, AH * 256).rearrange("p (h n) -> p h n", h=AH)
        st_at = cut(8704, 32).rearrange("p (s k b) -> p s k b", s=2, k=8)
        silu_f = cut(0, 512).rearrange("p (s n) -> p s n", s=2)
        gT = cut(512, HT_FFN * 256).rearrange("p (t n) -> p t n", t=HT_FFN)
        xf_half = cut(2560, 512).bitcast(F16).rearrange("p (c k n) -> p c k n", c=2, k=KT)
        w2_tern = halves[:, 0:HT_FFN * D]
        g_half = halves[:, HT_FFN * D:HT_FFN * D + 2048].rearrange("p (s c n) -> p s c n", s=4, c=2)
        smb = cut(8736, KT * B * P).rearrange("p (k b n) -> p k b n", k=KT, b=B)
        sumo = cut(9248, B * D).rearrange("p (b n) -> p b n", b=B)
        kv_z = w_mem[:].rearrange("p k n -> p (k n)").rearrange("p (b c) -> p b c", b=B)
        turns = cut(0, 2 * B * 512).rearrange("p (s b f) -> p s b f", s=2, b=B)
        frac = mid[:, 0:2 * B * 512].rearrange("p (s b f) -> p s b f", s=2, b=B)
        cs = cut(2048, 2 * 2 * B * 512).rearrange("p (s c b f) -> p s c b f", s=2, c=2, b=B)
        qf = [a.rearrange("p (c n) -> p c n", c=4) for a in (
            cut(6144, 1024), cut(7168, 1024), cut(8192, 1024), w_conv[:].rearrange("p w n -> p (w n)")[:, 0:1024])]
        pa = mid[:, 3840:6912].rearrange("p (s h c n) -> p s h c n", s=3, h=2, c=2)
        yv = mid[:, 7168:8704].rearrange("p (b n) -> p b n", b=B)
        ysc = mid[:, 2304:3840].rearrange("p (s b k n) -> p s b k n", s=2, b=B, k=8)
        ysg = cut(9216, 768).rearrange("p (s b k n) -> p s b k n", s=2, b=B, k=8)
        Y_BANKS = (0, 7, 1)
        yT = cut(0, 6 * 256).rearrange("p (t n) -> p t n", t=6)
        xe_half = halves[:, 0:1024].rearrange("p (c k n) -> p c k n", c=2, k=KT)
        gu_half = halves[:, 1024:3840].rearrange("p (s c k n) -> p s c k n", s=2, c=2, k=KT)
        H = cut(0, B * UNITS * EI).rearrange("p (b n) -> p b n", b=B)
        HT = cut(7040, 4 * 512).rearrange("p (s t b n) -> p s t b n", s=4, t=2, b=B)
        esg = cut(9088, 4 * EI).rearrange("p (s n) -> p s n", s=4)
        lg = cut(9792, B * 17).rearrange("p (b n) -> p b n", b=B)
        ex = cut(9832, B * 17).rearrange("p (b n) -> p b n", b=B)
        lmax = cut(9870, 2)
        top = cut(9872, B * 8).rearrange("p (b n) -> p b n", b=B)
        topi = cut(9888, B * 8).bitcast(U32).rearrange("p (b n) -> p b n", b=B)
        topf = cut(9904, B * 8).rearrange("p (b n) -> p b n", b=B)
        eq = w_mem[:].rearrange("p k n -> p (k n)")[:, 0:B * TOPK * E].rearrange("p (b k n) -> p b k n", b=B, k=TOPK)
        cw = cut(9920, B * UNITS).rearrange("p (b n) -> p b n", b=B)
        cws = cut(9960, 2)
        msk = cut(9964, B * E).rearrange("p (b n) -> p b n", b=B)

        def layer_norm(dve, k, add=None, src=x, normed=True):
            for b in range(B):
                if add:
                    add(b)
                step(dve, nc.vector.bn_stats(bn[:, b], src[:, b]))
                nc.vector.bn_aggr(mv[:, b], bn[:, b]).then_inc(sem("ln_stats"), 1)
            if not normed:
                dve.wait_ge(sem("ln_stats"), B * (k + 1))
            for b in range(B if normed else 0):
                dve.wait_ge(sem("ln_rstd"), B * k + b + 1)
                nc.vector.tensor_scalar(xn[:, b], src[:, b], mv[:, b, 0:1], rstd[:, b:b + 1], ALU.subtract,
                                        ALU.mult).then_inc(sem("ln_normed"), 1)

        def ln_copy(dve, n, bank):
            dve.wait_ge(sem("ln_transposed"), n + 1)
            nc.vector.tensor_copy(xnT[:, :, :, 3:], ps[:, bank].rearrange("p (k b l) -> p k b l", k=KT, b=B)
                                  ).then_inc(sem("xnT_ready"), 1)

        def split_x(dve, half, bank, name):
            t = ps[:, bank].rearrange("p (k n) -> p k n", k=KT)
            high = half[:, 0] if half.dtype == F16 else half[:, 0].bitcast(F32)
            nc.vector.tensor_copy(half[:, 0], t).then_inc(sem(name + "_high"), 1)
            dve.wait_ge(sem(name + "_high"), 1)
            nc.vector.tensor_tensor(half[:, 1], t, high, ALU.subtract).then_inc(sem(name + "_low"), 1)

        def ln_rstd(act, k):
            for b in range(B):
                act.wait_ge(sem("ln_stats"), B * k + b + 1)
                nc.scalar.activation(lnv[:, b:b + 1], mv[:, b, 1:2], ACT.Ln, bias=1e-5).then_inc(sem("ln_log"), 1)
                act.wait_ge(sem("ln_log"), B * k + b + 1)
                nc.scalar.activation(rstd[:, b:b + 1], lnv[:, b:b + 1], ACT.Exp, scale=-0.5).then_inc(sem("ln_rstd"), 1)

        def keep_warm(n, bank):
            o = ones[:].bitcast(F16)
            for _ in range(n):
                nc.tensor.matmul(ps[:, bank, 0:256], o[:, 0:P], o, start=True, stop=True)

        def ln_transpose(pe, k, bank):
            if k == LN_OF["attn"]:
                pe.wait_ge(sem("kv_taken"), NB)
                keep_warm(WARM[k], 6)
            elif k != LN_OF["xattn"]:
                keep_warm(WARM[k], 0)
            for b in range(B):
                pe.wait_ge(sem("ln_normed"), B * (k - (k > LN_OF["summary2"])) + b + 1)
                for kt in range(KT):
                    i = nc.tensor.transpose(ps[:, bank, (kt * B + b) * P:(kt * B + b + 1) * P],
                                            xn[:, b, kt * P:(kt + 1) * P], id32[:])
            i.then_inc(sem("ln_transposed"), 1)

        steps = [0]

        def step(dve, ins):
            steps[0] += 1
            ins.then_inc(sem("dve_step"), 1)
            dve.wait_ge(sem("dve_step"), steps[0])

        def tensor_attention(pe):
            T = nc.tensor
            ln_transpose(pe, LN_OF["attn"], 7)
            pe.wait_ge(sem("w_attn"), loaded["w_attn"])

            def project_values(i, b):
                if i or b:
                    pe.wait_ge(sem("v_copied"), 2 * (i // 4) + b)
                for kt in range(KT):
                    ins = T.matmul(ps[:, 2], xnT[:, kt, b, 3:], w_qkv[:, 2, kt, i * AD:(i + 4) * AD],
                                   start=(kt == 0), stop=(kt == KT - 1))
                ins.then_inc(sem("v_projected"), 1)

            for i in range(AH + 4):
                if i < AH:
                    if i >= 2:
                        pe.wait_ge(sem("qk_taken"), 2 * (i - 1))
                    pe.wait_ge(sem("qk_low"), i + 1)
                    for w in range(2):
                        for n, (c, d) in enumerate(HALF_PRODUCTS):
                            if i == w == 0 and n != 1:
                                pe.wait_ge(sem(("xa_high", None, "xa_low")[n]), 1)
                            for kt in range(KT):
                                ins = T.matmul(ps[:, i % 2, w * 256:w * 256 + 256], qk_half[:, i % 2, c, w, kt],
                                               xa_half[:, d, kt], start=(n + kt == 0), stop=(n == 2 and kt == KT - 1))
                    ins.then_inc(sem("qk_projected"), 1)
                if i == 0:
                    pe.wait_ge(sem("xnT_ready"), 2)
                if i < AH and i % 4 == 0:
                    project_values(i, 0)
                h = i - 1
                if 0 <= h < AH:
                    pe.wait_ge(sem("qk_taken"), 2 * (h + 1))
                    if h:
                        pe.wait_ge(sem("s_masked"), h)
                    for b in range(B):
                        ins = T.matmul(ps[:, 3, b * P:b * P + P], qT[:, h % 2, b * P:b * P + P],
                                       kT2[:, h % 2, b * P:b * P + P], start=True, stop=True)
                    ins.then_inc(sem("s_scored"), 1)
                h = i - 2
                if 0 <= h < AH:
                    pe.wait_ge(sem("p_normed"), h + 1)
                    if h:
                        pe.wait_ge(sem("pT_taken"), h)
                    for b in range(B):
                        ins = T.transpose(ps[:, 4, b * P:b * P + P], p_at[:, h % 2, b], id32[:])
                    ins.then_inc(sem("p_turned"), 1)
                h = i - 3
                if 0 <= h < AH:
                    pe.wait_ge(sem("pT_taken"), h + 1)
                    pe.wait_ge(sem("v_copied"), 2 * (h // 4 + 1))
                    if h:
                        pe.wait_ge(sem("o_taken"), h)
                    for b in range(B):
                        ins = T.matmul(ps[:, 5, b * P:b * P + P], v_at[:, (h // 4) % 2, b, (h % 4) * AD:(h % 4 + 1) * AD],
                                       pT_at[:, h % 2, b], start=True, stop=True)
                    ins.then_inc(sem("o_summed"), 1)
                if i < AH and i % 4 == 0:
                    project_values(i, 1)
                if i == 1:
                    pe.wait_ge(sem("u_ready"), 1)
                    for et in range(KT):
                        for kt in range(KT):
                            ins = T.matmul(ps[:, 6, et * B:et * B + B], w_in[:, kt, et * P:(et + 1) * P], usum[:, kt],
                                         start=(kt == 0), stop=(kt == KT - 1))
                    ins.then_inc(sem("state_summed"), 1)
                if i == AH - 2:
                    pe.wait_ge(sem("state_taken"), 1)
                    pe.wait_ge(sem("v_copied"), 2 * AH // 4)
                    pe.wait_ge(sem("w_sum"), loaded["w_sum"])
                    for b in range(B):
                        for kt in range(KT):
                            ins = T.matmul(ps[:, 2, b * D:(b + 1) * D], smb[:, kt, b], w_out1[:, kt], start=(kt == 0),
                                           stop=(kt == KT - 1))
                    ins.then_inc(sem("summary_ready"), 1)
                h = i - 4
                if 0 <= h < AH:
                    output_head(pe, h)

        def output_head(pe, h):
            pe.wait_ge(sem("o_taken"), h + 1)
            for b in range(B):
                ins = nc.tensor.matmul(ps[:, 6 + b, 0:D], oT_at[:, h, b * P:b * P + P], w_o[:, h],
                                       start=(h == 0), stop=(h == AH - 1))
                if h == AH - 1:
                    ins.then_inc(sem("attn_out"), 1)

        def head_weights(i):
            return w_qkv[:, 0:2, :, i * AD:(i + 1) * AD]

        def head_high(act, i):
            if i >= 2:
                act.wait_ge(sem("qk_projected"), i - 1)
            for w in range(2):
                nc.scalar.copy(qk_half[:, i % 2, 0, w], head_weights(i)[:, w]).then_inc(sem("qk_high"), 1)

        def pool_attention(pool):
            for i in range(AH):
                pool.wait_ge(sem("qk_high"), 2 * (i + 1))
                for w in range(2):
                    ins = nc.gpsimd.tensor_tensor(qk_half[:, i % 2, 1, w], head_weights(i)[:, w],
                                                  qk_half[:, i % 2, 0, w].bitcast(F32), ALU.subtract)
                    if w == 1:
                        ins.then_inc(sem("qk_low"), 1)

        def scalar_attention(act):
            act.wait_ge(sem("kv_projected"), NB)
            act.wait_ge(sem("w_attn"), loaded["w_attn"])
            for i in range(2):
                head_high(act, i)
            ln_rstd(act, LN_OF["attn"])
            act.wait_ge(sem("w_phase"), loaded["w_phase"])
            nc.scalar.activation(logw[:, 0], small[:, 0], ACT.Abs).then_inc(sem("slope_step"), 1)
            act.wait_ge(sem("slope_step"), 1)
            nc.scalar.activation(logw[:, 1], logw[:, 0], ACT.Exp, scale=-1.0).then_inc(sem("slope_step"), 1)
            act.wait_ge(sem("slope_step"), 2)
            nc.scalar.activation(logw[:, 2], logw[:, 1], ACT.Ln, bias=1.0).then_inc(sem("slope_log"), 1)

            def take_values(i, b):
                act.wait_ge(sem("v_projected"), 2 * (i // 4) + b + 1)
                if i >= 8:
                    act.wait_ge(sem("o_summed"), i - 4)
                nc.scalar.copy(v_at[:, (i // 4) % 2, b], ps[:, 2]).then_inc(sem("v_copied"), 1)

            for i in range(AH + 2):
                if i < AH and i % 4 == 0:
                    take_values(i, 0)
                h = i - 1
                if 0 <= h < AH:
                    act.wait_ge(sem("s_negmax"), h + 1)
                    if h >= 2:
                        act.wait_ge(sem("p_turned"), h - 1)
                    for b in range(B):
                        nc.scalar.activation(p_at[:, h % 2, b], s_at[:, h % 2, b], ACT.Exp,
                                             bias=st_at[:, h % 2, 0, b:b + 1],
                                             accum_out=st_at[:, h % 2, 1, b:b + 1]).then_inc(sem("p_exp"), 1)
                h = i - 2
                if 0 <= h < AH:
                    act.wait_ge(sem("p_turned"), h + 1)
                    if h >= 2:
                        act.wait_ge(sem("o_summed"), h - 1)
                    nc.scalar.copy(pT_at[:, h % 2], ps[:, 4, 0:256].rearrange("p (b n) -> p b n", b=B)
                                   ).then_inc(sem("pT_taken"), 1)
                if i < AH and i % 4 == 0:
                    take_values(i, 1)
                if i + 2 < AH:
                    head_high(act, i + 2)

        def vector_attention(dve, add_previous):
            V = nc.vector
            layer_norm(dve, LN_OF["attn"], add_previous)
            dve.wait_ge(sem("ln_transposed"), 2)
            split_x(dve, xa_half, 7, "xa")
            ln_copy(dve, 1, 7)
            dve.wait_ge(sem("ctx_weighted"), NB)
            step(dve, V.tensor_reduce(usum[:].rearrange("p k b -> p b k"), uacc, AX_X, ALU.add))
            step(dve, V.tensor_reduce(gsum[:], geo, AX_X, ALU.add))
            dve.wait_ge(sem("w_sum"), loaded["w_sum"])
            V.tensor_scalar(bg[:], b_in[:], gsum[:, 0:1], None, ALU.mult).then_inc(sem("u_ready"), 1)
            dve.wait_ge(sem("w_attn"), loaded["w_attn"])
            for i in range(AH + 3):
                h = i - 2
                if 0 <= h < AH:
                    dve.wait_ge(sem("p_exp"), 2 * (h + 1))
                    step(dve, V.reciprocal(st_at[:, h % 2, 2], st_at[:, h % 2, 1]))
                    V.tensor_tensor(p_at[:, h % 2], p_at[:, h % 2],
                                    st_at[:, h % 2, 2, :, None].to_broadcast([P, B, L]), ALU.mult
                                    ).then_inc(sem("p_normed"), 1)
                if i < AH:
                    dve.wait_ge(sem("qk_projected"), i + 1)
                    if i >= 2:
                        dve.wait_ge(sem("s_scored"), i - 1)
                    V.tensor_scalar(qT[:, i % 2], ps[:, i % 2, 0:256], b_qkv[:, 0, i:i + 1], AD ** -0.5, ALU.add,
                                    ALU.mult).then_inc(sem("qk_taken"), 1)
                    V.tensor_scalar(kT2[:, i % 2], ps[:, i % 2, 256:512], b_qkv[:, 1, i:i + 1], None, ALU.add
                                    ).then_inc(sem("qk_taken"), 1)
                h = i - 1
                if 0 <= h < AH:
                    dve.wait_ge(sem("s_scored"), h + 1)
                    if h >= 2:
                        dve.wait_ge(sem("p_exp"), 2 * (h - 1))
                    V.tensor_tensor(s_at[:, h % 2], ps[:, 3, 0:256].rearrange("p (b n) -> p b n", b=B),
                                    mask[:, None, :].to_broadcast([P, B, L]), ALU.add).then_inc(sem("s_masked"), 1)
                    dve.wait_ge(sem("s_masked"), h + 1)
                    V.tensor_reduce(st_at[:, h % 2, 0], s_at[:, h % 2], AX_X, ALU.max, negate=True
                                    ).then_inc(sem("s_negmax"), 1)
                h = i - 3
                if 0 <= h < AH:
                    dve.wait_ge(sem("o_summed"), h + 1)
                    V.tensor_scalar(oT_at[:, h], ps[:, 5, 0:256], b_qkv[:, 2, h:h + 1], None, ALU.add
                                    ).then_inc(sem("o_taken"), 1)
                if i == 2:
                    dve.wait_ge(sem("state_summed"), 1)
                    for et in range(KT):
                        step(dve, V.tensor_scalar(smean[:, et], ps[:, 6, et * B:et * B + B], bg[:, et:et + 1], 1.0 / M,
                                                  ALU.add, ALU.mult))
                    V.tensor_copy(smb, smean[:, :, :, None].to_broadcast([P, KT, B, P])).then_inc(sem("state_taken"), 1)
                if i == AH // 2:
                    dve.wait_ge(sem("slope_log"), 1)
                    step(dve, V.tensor_scalar(logw[:, 3], small[:, 0], 0.0, None, ALU.max))
                    step(dve, V.tensor_tensor(logw[:, 4], logw[:, 3], logw[:, 2], ALU.add))
                    step(dve, V.tensor_tensor(logw[:, 5], logw[:, 4], small[:, 2], ALU.mult))
                    for b in range(B):
                        step(dve, V.tensor_tensor(x[:, b], x[:, b], b_o[:], ALU.add))
                if i == AH + 1:
                    dve.wait_ge(sem("summary_ready"), 1)
                    step(dve, V.tensor_tensor(sumo, ps[:, 2].rearrange("p (b n) -> p b n", b=B),
                                              vecs[:, 0:1, :].to_broadcast([P, B, D]), ALU.add))

            def add(b):
                dve.wait_ge(sem("attn_out"), b + 1)
                step(dve, V.tensor_tensor(x[:, b], x[:, b], ps[:, 6 + b, 0:D], ALU.add))
            return add

        def tensor_ffn(pe):
            T = nc.tensor
            ln_transpose(pe, LN_OF["ffn"], 0)
            pe.wait_ge(sem("ffn_quarters"), 13)
            for j in range(HT_FFN + 2):
                if j < HT_FFN:
                    if j >= 4:
                        pe.wait_ge(sem("g_ready"), j - 3)
                    for w in range(2):
                        for n, (c, kt) in enumerate((c, kt) for c in range(2) for kt in range(KT)):
                            if j == w == kt == 0:
                                pe.wait_ge(sem(("xf_high", "xf_low")[c]), 1)
                            i = T.matmul(ps[:, 1 + j % 4, w * 256:w * 256 + 256],
                                         w_tern[:, w, kt * HT_FFN * P + j * P:kt * HT_FFN * P + (j + 1) * P],
                                         xf_half[:, c, kt], start=(n == 0), stop=(n == 2 * KT - 1))
                    i.then_inc(sem("h_projected"), 1)
                t = j - 2
                if t >= 0:
                    pe.wait_ge(sem("g_split"), t + 1)
                    pe.wait_ge(sem("w2_ready"), 1)
                    for b in range(B):
                        for c in range(2):
                            i = T.matmul(ps[:, 5 + b, 0:D], g_half[:, t % 4, c, b * P:b * P + P],
                                         w2_tern[:, t * D:(t + 1) * D], start=(t + c == 0), stop=(t == HT_FFN - 1 and c == 1))
                    i.then_inc(sem("g_used"), 1)

        def scalar_ffn(act):
            ln_rstd(act, LN_OF["ffn"])
            nc.scalar.preload_act_table_set("silu_and_others")
            act.wait_ge(sem("qk_projected"), AH)
            nc.scalar.copy(w2_tern, w_tern[:, 2]).then_inc(sem("w2_ready"), 1)
            for j in range(HT_FFN + 1):
                if j < HT_FFN:
                    act.wait_ge(sem("h_projected"), j + 1)
                    if j >= 2:
                        act.wait_ge(sem("g_ready"), j - 1)
                    nc.scalar.activation(silu_f[:, j % 2], ps[:, 1 + j % 4, 0:256], ACT.Silu, scale=fsc[:, 3:4]
                                         ).then_inc(sem("h_gated"), 1)
                t = j - 1
                if t >= 0:
                    act.wait_ge(sem("g_ready"), t + 1)
                    if t >= 4:
                        act.wait_ge(sem("g_used"), t - 3)
                    nc.scalar.copy(g_half[:, t % 4, 0], gT[:, t]).then_inc(sem("g_high"), 1)

        def vector_ffn(dve, add_previous):
            V = nc.vector
            layer_norm(dve, LN_OF["ffn"], add_previous)
            dve.wait_ge(sem("ln_transposed"), 3)
            split_x(dve, xf_half, 0, "xf")
            for j in range(HT_FFN + 1):
                if j < HT_FFN:
                    dve.wait_ge(sem("h_gated"), j + 1)
                    V.scalar_tensor_tensor(gT[:, j], ps[:, 1 + j % 4, 256:512], fsc[:, 4:5], silu_f[:, j % 2], ALU.mult,
                                           ALU.mult).then_inc(sem("g_ready"), 1)
                t = j - 1
                if t >= 0:
                    dve.wait_ge(sem("g_high"), t + 1)
                    V.tensor_tensor(g_half[:, t % 4, 1], gT[:, t], g_half[:, t % 4, 0].bitcast(F32), ALU.subtract
                                    ).then_inc(sem("g_split"), 1)
            dve.wait_ge(sem("g_used"), HT_FFN)

            def add(b):
                step(dve, V.scalar_tensor_tensor(x[:, b], ps[:, 5 + b, 0:D], fsc[:, 5:6], x[:, b], ALU.mult, ALU.add))
            return add

        def vector_summary(dve, add_previous):
            V = nc.vector
            layer_norm(dve, LN_OF["summary"], add_previous)

            def add_summary(b):
                dve.wait_ge(sem("ln_normed"), B * LN_OF["summary"] + b + 1)
                step(dve, V.tensor_tensor(xn[:, b], xn[:, b], sumo[:, b], ALU.add))
            layer_norm(dve, LN_OF["summary2"], add_summary, xn, normed=False)

            def add(b):
                step(dve, V.scalar_tensor_tensor(xn[:, b], xn[:, b], mv[:, b, 0:1], vecs[:, 1], ALU.subtract, ALU.mult))
                dve.wait_ge(sem("ln_rstd"), B * LN_OF["summary2"] + b + 1)
                dve.wait_ge(sem("beta_added"), b + 1)
                step(dve, V.scalar_tensor_tensor(x[:, b], xn[:, b], rstd[:, b:b + 1], x[:, b], ALU.mult, ALU.add))
            return add

        def scalar_summary(act):
            nc.scalar.preload_act_table_set("natural_log_exp_and_others")
            ln_rstd(act, LN_OF["summary"])
            ln_rstd(act, LN_OF["summary2"])

        def tensor_phase(pe):
            T = nc.tensor
            ln_transpose(pe, LN_OF["phase"], 0)
            pe.wait_ge(sem("xnT_ready"), 3)
            pe.wait_ge(sem("w_cm_ready"), KT)
            for b in range(B):
                for n, (kt, w) in enumerate((kt, w) for kt in range(KT) for w in range(CONV)):
                    i = T.matmul(ps[:, 1 + b, 0:288], xnT[:, kt, b, w:w + L], w_cm[:, kt, w], start=(n == 0),
                                 stop=(n == KT * CONV - 1))
                i.then_inc(sem("z_ready"), 1)
            pe.wait_ge(sem("late_loaded"), 48)
            for kq in range(4):
                for c in range(2):
                    for kt in range(KT):
                        i = T.matmul(ps[:, 3 + kq, c * 256:c * 256 + 256],
                                     w_q4[:, kt, (2 * kq + c) * P:(2 * kq + c + 1) * P], xnT[:, kt, :, 3:],
                                     start=(kt == 0), stop=(kt == KT - 1))
                i.then_inc(sem("q4_projected"), 1)
            pe.wait_ge(sem("pw_ready"), 1)
            T.matmul(ps[:, 7, 0:B * 32], tri[:], pw[:].rearrange("p b k -> p (b k)"), start=True, stop=True
                     ).then_inc(sem("den_summed"), 1)
            pe.wait_ge(sem("logp_ready"), 1)
            pe.wait_ge(sem("w_ri_ready"), 2)
            for j in range(FT + 2):
                if j < FT:
                    kq, jj = j // 4, j % 4
                    if kq:
                        pe.wait_ge(sem("re_weighted"), kq)
                    else:
                        pe.wait_ge(sem("first_re_weighted"), 1)
                    pe.wait_ge(sem("im_weighted"), kq + 1)
                    if j >= 2:
                        pe.wait_ge(sem("state_used"), 2 * (j - 1))
                    for c in range(2):
                        for b in range(B):
                            i = T.matmul(ps[:, 1 + j % 2, (c * B + b) * P:(c * B + b + 1) * P],
                                         cs[:, kq % 2, c, b, jj * P:(jj + 1) * P], tri[:], start=True, stop=True)
                    i.then_inc(sem("state_ready"), 1)
                t = j - 2
                if t >= 0:
                    kq, jj = t // 4, t % 4
                    pe.wait_ge(sem("out_re"), t + 1)
                    pe.wait_ge(sem("state_used"), 2 * t + 2)
                    if kq >= 2:
                        pe.wait_ge(sem("out_im"), t - 7)
                    if t == 0:
                        pe.wait_ge(sem("q4_taken"), 6)
                    if t == 4:
                        pe.wait_ge(sem("q4_taken"), 12)
                    if jj == 0 and kq >= 2:
                        pe.wait_ge(sem("y_scaled"), B * (kq - 1))
                    for b in range(B):
                        parts = ((1, 0), (1, 1), (0, 0)) if kq < 2 else ((1, 0), (0, 0))
                        for n, (c, h) in enumerate(parts):
                            i = T.matmul(ps[:, 3 + 2 * (kq % 2) + b, jj * 96:jj * 96 + 96],
                                         pa[:, t % 3, c, h, b * P:b * P + P], w_ri[:, c, t], start=(n == 0), stop=(n == len(parts) - 1))
                    i.then_inc(sem("y_summed"), 1)

            def turn_y(t):
                for u in range(2):
                    for b in range(B):
                        i = T.transpose(ps[:, Y_BANKS[t], (u * B + b) * P:(u * B + b + 1) * P],
                                        yv[:, b, (2 * t + u) * P:(2 * t + u + 1) * P], id32[:])
                i.then_inc(sem("y_turned"), 1)

            def sum_y(t):
                pe.wait_ge(sem("yT_taken"), t + 1)
                for b in range(B):
                    for u in range(2 * t, 2 * t + 2):
                        i = T.matmul(ps[:, 3 + b, 0:D], yT[:, u, b * P:b * P + P], w_out2[:, u], start=(u == 0), stop=(u == 5))
                    if t == 2:
                        i.then_inc(sem("phase_out"), 1)

            pe.wait_ge(sem("y_gated"), 2 * B)
            turn_y(0)
            pe.wait_ge(sem("y_gated"), 3 * B)
            turn_y(1)
            pe.wait_ge(sem("y_scaled"), 3 * B)
            sum_y(0)
            pe.wait_ge(sem("last_y_gated"), B)
            pe.wait_ge(sem("state_used"), 2 * FT)
            turn_y(2)
            sum_y(1)
            sum_y(2)

        def vector_phase(dve, add_previous):
            V = nc.vector
            layer_norm(dve, LN_OF["phase"], add_previous)
            ln_copy(dve, 3, 0)

            def turn(kq, b):
                return V.scalar_tensor_tensor(turns[:, kq % 2, b].rearrange("p (k m) -> p k m", m=CM),
                                              kv_z[:, b, kq * 64:kq * 64 + 64, None].to_broadcast([P, 64, CM]),
                                              1.0 / TWO_PI,
                                              theta[:, kq * 512:kq * 512 + 512].rearrange("p (k m) -> p k m", m=CM),
                                              ALU.mult, ALU.mult)

            def nearest(kq):
                s = kq % 2
                return V.tensor_scalar(frac[:, s], turns[:, s], ROUND_MAGIC, ROUND_MAGIC, ALU.add, ALU.subtract)

            def fraction(kq):
                s = kq % 2
                V.tensor_tensor(frac[:, s], turns[:, s], frac[:, s], ALU.subtract).then_inc(sem("frac_ready"), 1)

            def scale_y(kq, b):
                dve.wait_ge(sem("y_summed"), 4 * kq + 4)
                if kq >= 2:
                    dve.wait_ge(sem("y_gated"), B * (kq - 1))
                V.tensor_tensor(ysc[:, kq % 2, b], ps[:, 3 + 2 * (kq % 2) + b, 0:384].rearrange("p (k n) -> p k n", n=SW),
                                iden[:, b, kq * 8:kq * 8 + 8, None].to_broadcast([P, 8, SW]), ALU.mult
                                ).then_inc(sem("y_scaled"), 1)

            def take_y(t):
                dve.wait_ge(sem("y_turned"), t + 1)
                V.tensor_copy(yT[:, 2 * t:2 * t + 2], ps[:, Y_BANKS[t]].rearrange("p (u n) -> p u n", u=2)
                              ).then_inc(sem("yT_taken"), 1)

            for b in range(B):
                dve.wait_ge(sem("z_ready"), b + 1)
                step(dve, V.tensor_copy(kv_z[:, b], ps[:, 1 + b, 0:288]))
                if b == 0:
                    dve.wait_ge(sem("late_loaded"), 48)
                    step(dve, turn(0, 0))
            step(dve, V.tensor_tensor(pw[:], kv_z[:, :, 256:288], small[:, 1:2, :].to_broadcast([P, B, 32]), ALU.mult))
            step(dve, V.tensor_scalar(pw[:], pw[:], 20.0, -20.0, ALU.min, ALU.max))
            V.tensor_tensor(pw[:], pw[:], logw[:, 5:6, :].to_broadcast([P, B, 32]), ALU.add).then_inc(sem("logp_ready"), 1)
            step(dve, turn(0, 1))
            step(dve, nearest(0))
            fraction(0)
            for b in range(B):
                i = turn(1, b)
            step(dve, i)
            step(dve, nearest(1))
            fraction(1)
            dve.wait_ge(sem("cos_ready"), 1)
            r = cs[:, 0, 0].rearrange("p b (k n) -> p b k n", n=64)
            V.tensor_tensor(r, r, pw[:, :, 0:8, None].to_broadcast([P, B, 8, 64]), ALU.mult
                            ).then_inc(sem("first_re_weighted"), 1)
            dve.wait_ge(sem("den_summed"), 1)
            step(dve, V.tensor_scalar(iden[:], ps[:, 7, 0:B * 32].rearrange("p (b k) -> p b k", b=B), 1e-4, None, ALU.max))
            step(dve, V.reciprocal(iden[:], iden[:]))
            for j in range(FT):
                kq, jj = j // 4, j % 4
                dve.wait_ge(sem("state_ready"), j + 1)
                if j >= 3:
                    dve.wait_ge(sem("y_summed"), j - 2)
                if jj == 0:
                    dve.wait_ge(sem("q4_taken"), 3 * (kq + 1))
                for c in range(2):
                    V.tensor_tensor(pa[:, j % 3, c], ps[:, 1 + j % 2].rearrange("p (c n) -> p c n", c=2),
                                    qf[kq][:, 2 * c:2 * c + 2], ALU.mult).then_inc(sem("state_used"), 1)
                if kq >= 2:
                    dve.wait_ge(sem("state_used"), 2 * j + 2)
                    V.tensor_tensor(pa[:, j % 3, 1, 0], pa[:, j % 3, 1, 0], pa[:, j % 3, 1, 1], ALU.add
                                    ).then_inc(sem("out_im"), 1)
                if kq < 2 and jj == 0:
                    dve.wait_ge(sem("cos_ready"), kq + 1)
                    for b in range(B):
                        i = turn(kq + 2, b)
                    step(dve, i)
                if kq < 2 and jj == 1:
                    nearest(kq + 2).then_inc(sem("nearest_ready"), 1)
                if kq and jj in (1, 3):
                    scale_y(kq - 1, jj // 2)
            for b in range(B):
                scale_y(3, b)
            take_y(0)
            dve.wait_ge(sem("y_silu"), 4)
            for b in range(B):
                V.tensor_tensor(yv[:, b, 576:768].rearrange("p (k n) -> p k n", n=24), ysc[:, 1, b, :, 0:24], ysg[:, 1, b],
                                ALU.mult).then_inc(sem("last_y_gated"), 1)
            for t in range(1, 3):
                take_y(t)

            def add(b):
                dve.wait_ge(sem("phase_out"), b + 1)
                step(dve, V.tensor_tensor(x[:, b], x[:, b], ps[:, 3 + b, 0:D], ALU.add))
            return add

        def scalar_phase(act):
            ln_rstd(act, LN_OF["phase"])
            act.wait_ge(sem("logp_ready"), 1)
            nc.scalar.activation(pw[:], pw[:], ACT.Exp).then_inc(sem("pw_ready"), 1)

            def waves(kq):
                s = kq % 2
                if kq < 2:
                    act.wait_ge(sem("frac_ready"), kq + 1)
                else:
                    act.wait_ge(sem("late_frac_ready"), kq - 1)
                if kq >= 2:
                    act.wait_ge(sem("state_ready"), 4 * (kq - 1))
                nc.scalar.activation(cs[:, s, 1], frac[:, s], ACT.Sin, scale=TWO_PI).then_inc(sem("sin_ready"), 1)
                nc.scalar.activation(turns[:, s], frac[:, s], ACT.Abs).then_inc(sem("abs_ready"), 1)
                act.wait_ge(sem("abs_ready"), kq + 1)
                nc.scalar.activation(cs[:, s, 0], turns[:, s], ACT.Sin, scale=-TWO_PI, bias=math.pi / 2
                                     ).then_inc(sem("cos_ready"), 1)

            def silu_y(kq):
                act.wait_ge(sem("y_scaled"), B * (kq + 1))
                if kq >= 2:
                    act.wait_ge(sem("y_gated"), B * (kq - 1))
                nc.scalar.activation(ysg[:, kq % 2], ysc[:, kq % 2, :, :, 24:48], ACT.Silu).then_inc(sem("y_silu"), 1)

            nc.scalar.preload_act_table_set("silu_and_others")
            def take_queries(kq):
                act.wait_ge(sem("q4_projected"), kq + 1)
                nc.scalar.copy(qf[kq][:, 0:2], ps[:, 3 + kq].rearrange("p (c n) -> p c n", c=2)).then_inc(sem("q4_taken"), 1)
                nc.scalar.activation(qf[kq][:, 2], ps[:, 3 + kq, 256:512], ACT.Copy, scale=-1.0).then_inc(sem("q4_taken"), 1)
                nc.scalar.copy(qf[kq][:, 3], ps[:, 3 + kq, 0:256]).then_inc(sem("q4_taken"), 1)

            waves(0)
            for kq in range(2):
                take_queries(kq)
            waves(1)
            for kq in range(2, 4):
                take_queries(kq)
            waves(2)
            silu_y(0)
            waves(3)
            for kq in range(1, 4):
                silu_y(kq)
            nc.scalar.preload_act_table_set("natural_log_exp_and_others")

        def pool_phase(pool):
            G = nc.gpsimd
            def weigh(kq, c, made, weighted):
                pool.wait_ge(sem(made), kq + 1)
                if kq == 0:
                    pool.wait_ge(sem("pw_ready"), 1)
                r = cs[:, kq % 2, c].rearrange("p b (k n) -> p b k n", n=64)
                G.tensor_tensor(r, r, pw[:, :, kq * 8:kq * 8 + 8, None].to_broadcast([P, B, 8, 64]), ALU.mult
                                ).then_inc(sem(weighted), 1)

            def gate_y(kq):
                pool.wait_ge(sem("y_silu"), kq + 1)
                for b in range(B):
                    G.tensor_tensor(yv[:, b, kq * 192:kq * 192 + 192].rearrange("p (k n) -> p k n", n=24),
                                    ysc[:, kq % 2, b, :, 0:24], ysg[:, kq % 2, b], ALU.mult).then_inc(sem("y_gated"), 1)

            weigh(0, 1, "sin_ready", "im_weighted")
            for j in range(FT):
                kq, jj = j // 4, j % 4
                pool.wait_ge(sem("state_used"), 2 * j + 1)
                G.tensor_tensor(pa[:, j % 3, 0, 0], pa[:, j % 3, 0, 0], pa[:, j % 3, 0, 1], ALU.add
                                ).then_inc(sem("out_re"), 1)
                if jj == 2 and kq < 2:
                    pool.wait_ge(sem("nearest_ready"), kq + 1)
                    G.tensor_tensor(frac[:, kq % 2], turns[:, kq % 2], frac[:, kq % 2], ALU.subtract
                                    ).then_inc(sem("late_frac_ready"), 1)
                if jj == 0 and kq < 3:
                    weigh(kq + 1, 1, "sin_ready", "im_weighted")
                if jj == 1 and kq < 3:
                    weigh(kq + 1, 0, "cos_ready", "re_weighted")
                if jj == 3 and 1 <= kq < 3:
                    gate_y(kq - 1)
            gate_y(2)

        def tensor_experts(pe):
            T = nc.tensor
            ln_transpose(pe, LN_OF["moe"], 0)
            pe.wait_ge(sem("xnT_ready"), 4)
            pe.wait_ge(sem("w_moe"), loaded["w_moe"])
            for b in range(B):
                for kt in range(KT):
                    i = T.matmul(ps[:, 1, b * 32:b * 32 + 17], xnT[:, kt, b, 3:], w_rt[:, kt], start=(kt == 0),
                                 stop=(kt == KT - 1))
            i.then_inc(sem("routed"), 1)
            turned = 0
            summed = 0

            def turn(n):
                last = min(DT, 2 * n + 2) - 1
                need = (min(UNITS * EI, (last + 1) * P) - 1) // EI + 1
                pe.wait_ge(sem("h_ready"), B * need)
                if n >= 2:
                    pe.wait_ge(sem("HT_taken"), n - 1)
                for u in range(2):
                    w = min(P, UNITS * EI - (2 * n + u) * P)
                    for b in range(B):
                        i = T.transpose(ps[0:w, 6 + n % 2, (u * B + b) * P:(u * B + b + 1) * P],
                                        H[:, b, (2 * n + u) * P:(2 * n + u) * P + w], id32[:])
                i.then_inc(sem("H_turned"), 1)

            def down(n):
                pe.wait_ge(sem("HT_taken"), n + 1)
                if n == 0:
                    pe.wait_ge(sem("down_loaded"), 16)
                    pe.wait_ge(sem("logits_taken"), 1)
                for b in range(B):
                    for u in range(2):
                        t = 2 * n + u
                        w = min(P, UNITS * EI - t * P)
                        i = T.matmul(ps[:, b, 0:D], HT[0:w, n % 4, u, b], w_down[0:w, t], start=(t == 0), stop=(t == DT - 1))
                    i.then_inc(sem("downed"), 1)

            for k in range(B * UNITS):
                u, b = k // B, k % B
                if k >= 4:
                    pe.wait_ge(sem("h_ready"), k - 3)
                if b == 0:
                    pe.wait_ge(sem("gu_low"), u + 1)
                for n, (d, c) in enumerate(HALF_PRODUCTS):
                    if k == 0 and n != 1:
                        pe.wait_ge(sem(("xe_high", None, "xe_low")[n]), 1)
                    for kt in range(KT):
                        i = T.matmul(ps[:, 2 + k % 4, 0:2 * EI], xe_half[:, c, kt, b * P:b * P + P], gu_half[:, u % 2, d, kt],
                                     start=(n + kt == 0), stop=(n == 2 and kt == KT - 1))
                i.then_inc(sem("gu_projected"), 1)
                if b == B - 1:
                    while turned < DT // 2 and (2 * turned + 2) * P <= (u - 1) * EI:
                        turn(turned)
                        turned += 1
                        if turned >= 2:
                            down(summed)
                            summed += 1
            while turned < DT // 2:
                turn(turned)
                turned += 1
                down(summed)
                summed += 1
            while summed < DT // 2:
                down(summed)
                summed += 1

        def unit_high(act, u):
            if u >= 2:
                act.wait_ge(sem("gu_projected"), B * (u - 1))
            nc.scalar.copy(gu_half[:, u % 2, 0], w_gu[:, :, u * 2 * EI:(u + 1) * 2 * EI]).then_inc(sem("gu_high"), 1)

        def pool_experts(pool):
            for u in range(UNITS):
                pool.wait_ge(sem("gu_high"), u + 1)
                nc.gpsimd.tensor_tensor(gu_half[:, u % 2, 1], w_gu[:, :, u * 2 * EI:(u + 1) * 2 * EI],
                                        gu_half[:, u % 2, 0].bitcast(F32), ALU.subtract).then_inc(sem("gu_low"), 1)

        def scalar_experts(act):
            act.wait_ge(sem("gu_loaded"), 16 * KT)
            for u in range(2):
                unit_high(act, u)
            ln_rstd(act, LN_OF["moe"])
            act.wait_ge(sem("lg_shifted"), 1)
            nc.scalar.activation(ex[:, :, 0:16], ex[:, :, 0:16], ACT.Exp).then_inc(sem("routes_exp"), 1)
            nc.scalar.activation(ex[:, :, 16:17], lg[:, :, 16:17], ACT.Exp, scale=-1.0).then_inc(sem("routes_exp"), 1)
            nc.scalar.preload_act_table_set("silu_and_others")
            evac = 0
            for k in range(B * UNITS):
                act.wait_ge(sem("gu_projected"), k + 1)
                if k >= 4:
                    act.wait_ge(sem("h_ready"), k - 3)
                nc.scalar.activation(esg[:, k % 4], ps[:, 2 + k % 4, 0:EI], ACT.Silu).then_inc(sem("g_gated"), 1)
                if k % B == B - 1:
                    u = k // B
                    if u + 2 < UNITS:
                        unit_high(act, u + 2)
                    while evac < DT // 2 and (2 * evac + 2) * P <= (u - 1) * EI:
                        take_H(act, evac)
                        evac += 1
            while evac < DT // 2:
                take_H(act, evac)
                evac += 1

        def take_H(act, n):
            act.wait_ge(sem("H_turned"), n + 1)
            if n >= 4:
                act.wait_ge(sem("downed"), B * (n - 3))
            if n < DT // 2 - 1:
                nc.scalar.copy(HT[:, n % 4].rearrange("p t b n -> p (t b n)"), ps[:, 6 + n % 2]).then_inc(sem("HT_taken"), 1)
            else:
                w = UNITS * EI - (DT - 1) * P
                nc.scalar.copy(HT[:, n % 4, 0].rearrange("p b n -> p (b n)"), ps[:, 6 + n % 2, 0:256]
                               ).then_inc(sem("HT_last"), 1)
                nc.scalar.copy(HT[0:w, n % 4, 1].rearrange("p b n -> p (b n)"), ps[0:w, 6 + n % 2, 256:512]
                               ).then_inc(sem("HT_taken"), 1)

        def vector_experts(dve, add_previous):
            V = nc.vector
            layer_norm(dve, LN_OF["moe"], add_previous)
            ln_copy(dve, 4, 0)
            split_x(dve, xe_half, 0, "xe")
            dve.wait_ge(sem("routed"), 1)
            V.tensor_copy(lg, ps[:, 1, 0:64].rearrange("p (b n) -> p b n", b=B)[:, :, 0:17]).then_inc(sem("logits_taken"), 1)
            dve.wait_ge(sem("logits_taken"), 1)
            step(dve, V.tensor_reduce(lmax, lg[:, :, 0:16], AX_X, ALU.max))
            V.tensor_tensor(ex[:, :, 0:16], lg[:, :, 0:16], lmax[:, :, None].to_broadcast([P, B, 16]), ALU.subtract
                            ).then_inc(sem("lg_shifted"), 1)
            dve.wait_ge(sem("routes_exp"), 2)
            for b in range(B):
                step(dve, V.max(top[:, b], ex[:, b, 0:16]))
                step(dve, V.max_index(topi[:, b], top[:, b], ex[:, b, 0:16]))
            step(dve, V.tensor_copy(topf, topi))
            step(dve, V.tensor_tensor(eq, iota[:, None, None, :].to_broadcast([P, B, TOPK, E]),
                                      topf[:, :, 0:TOPK, None].to_broadcast([P, B, TOPK, E]), ALU.is_equal))
            step(dve, V.tensor_reduce(msk, eq.rearrange("p b k n -> p b n k"), AX_X, ALU.add))
            step(dve, V.tensor_tensor(msk, msk, ex[:, :, 0:16], ALU.mult))
            step(dve, V.tensor_reduce(cws, msk, AX_X, ALU.add))
            step(dve, V.reciprocal(cws, cws))
            step(dve, V.tensor_tensor(cw[:, :, 0:E], msk, cws[:, :, None].to_broadcast([P, B, E]), ALU.mult))
            step(dve, V.tensor_scalar(ex[:, :, 16:17], ex[:, :, 16:17], 1.0, None, ALU.add))
            step(dve, V.reciprocal(ex[:, :, 16:17], ex[:, :, 16:17]))
            step(dve, V.tensor_copy(cw[:, :, E:UNITS], ex[:, :, 16:17].to_broadcast([P, B, 4])))
            for k in range(B * UNITS):
                u, b = k // B, k % B
                dve.wait_ge(sem("g_gated"), k + 1)
                V.scalar_tensor_tensor(H[:, b, u * EI:(u + 1) * EI], ps[:, 2 + k % 4, EI:2 * EI], cw[:, b, u:u + 1],
                                       esg[:, k % 4], ALU.mult, ALU.mult).then_inc(sem("h_ready"), 1)
            for b in range(B):
                dve.wait_ge(sem("downed"), B * (DT // 2 - 1) + b + 1)
                V.tensor_tensor(x[:, b], x[:, b], ps[:, b, 0:D], ALU.add).then_inc(sem("x_final"), 1)

        def tensor_rest(pe):
            for part in (tensor_attention, tensor_ffn, tensor_phase, tensor_experts):
                part(pe)

        def scalar_rest(act):
            for part in (scalar_attention, scalar_ffn, scalar_summary, scalar_phase, scalar_experts):
                part(act)

        def vector_rest(dve, add_context):
            add = add_context
            for part in (vector_attention, vector_ffn, vector_summary, vector_phase, vector_experts):
                add = part(dve, add)

        def pool_rest(pool):
            G = nc.gpsimd
            pool_attention(pool)
            pool.wait_ge(sem("w_phase"), loaded["w_phase"])
            pool.wait_ge(sem("w_ri_loaded"), 16)
            for c in range(2):
                G.tensor_tensor(w_ri[:, c], w_ri[:, c], w_nrm[:, :, None].to_broadcast([P, FT, 96]), ALU.mult
                                ).then_inc(sem("w_ri_ready"), 1)
            pool.wait_ge(sem("attn_out"), B)
            for kt in range(KT):
                G.tensor_tensor(w_cm[:, kt], w_mem[:, kt, None, :].to_broadcast([P, CONV, 288]), w_conv[:], ALU.mult
                                ).then_inc(sem("w_cm_ready"), 1)
            for b in range(B):
                pool.wait_ge(sem("ln_normed"), B * LN_OF["summary"] + b + 1)
                G.tensor_tensor(x[:, b], x[:, b], vecs[:, 2], ALU.add).then_inc(sem("beta_added"), 1)
            pool_phase(pool)
            pool_experts(pool)
        @block.vector
        def _(dve):
            V = nc.vector
            V.memset(ones[:], 1.0).then_inc(sem("ones_set"), 1)
            V.memset(zer, 0.0).then_inc(sem("zeros_set"), 1)
            V.memset(xnT[:, :, :, 0:3], 0.0)
            V.memset(v_sb[:, :, :, 8:9], 1.0)
            dve.wait_ge(sem("x_loaded"), 32)
            layer_norm(dve, LN_OF["xattn"])
            ln_copy(dve, 0, 0)
            dve.wait_ge(sem("decay_exp"), 1)
            step(dve, V.tensor_scalar(dec[:, 1:2], dec[:, 0:1], 1.0, None, ALU.add))
            step(dve, V.reciprocal(dec[:, 2:3], dec[:, 1:2]))
            V.tensor_tensor_scan(geo, dec[:, 2:3].to_broadcast([P, M]), ones[:, 0:1].to_broadcast([P, M]),
                                 0.0, ALU.mult, ALU.add).then_inc(sem("geo_ready"), 1)

            def copy_q(b):
                dve.wait_ge(sem("q_projected"), b + 1)
                V.tensor_copy(qraw[:, b], ps[:, 1 + b, 0:256]).then_inc(sem("q_copied"), 1)

            def mean_squares_q(b):
                dve.wait_ge(sem("q_squared"), b + 1)
                V.tensor_reduce(qms[:, b], qsq[:, b].rearrange("p (h d) -> p h d", d=XD), AX_X, ALU.add
                                ).then_inc(sem("q_meansq"), 1)

            def pack_q(b):
                dve.wait_ge(sem("q_rstd"), b + 1)
                qn = xn[:, b]
                step(dve, V.tensor_tensor(qn.rearrange("p (h d) -> p h d", d=XD),
                                          qraw[:, b].rearrange("p (h d) -> p h d", d=XD),
                                          qrs[:, b, :, None].to_broadcast([P, XH, XD]), ALU.mult))
                pack = qpack[:, b].rearrange("p (h s r d) -> p h s r d", s=2, r=2, d=XD)
                qn2 = qn.rearrange("p (h d) -> p h d", d=XD)[:, :, None, :].to_broadcast([P, XH, 2, XD])
                step(dve, V.tensor_copy(pack[:, :, 0], qn2))
                V.tensor_tensor(pack[:, :, 1], qn2, pack[:, :, 0], ALU.subtract).then_inc(sem("q_packed"), 1)

            def take_q(b, bank):
                dve.wait_ge(sem("q_transposed"), b + 1)
                if b == 0:
                    dve.wait_ge(sem("qbd_zero"), 1)
                t = ps[:, bank].bitcast(F16).rearrange("p (g n) -> p g n", g=GROUPS)
                for j in range(4):
                    rows = slice(32 * j, 32 * j + 32)
                    i = V.tensor_copy(qbd[rows, b, :, (j % 2) * P:(j % 2 + 1) * P], t[rows])
                i.then_inc(sem("q_ready"), 1)

            def take_kv(t, s):
                dve.wait_ge(sem("kv_projected"), t + 1)
                V.tensor_copy(kraw[:, s % 2], ps[:, 6, 0:256]).then_inc(sem("k_taken"), 1)
                if not (isinstance(t, int) and t < V_SLOTS):
                    dve.wait_ge(sem("pv_done"), 4 * t - 12)
                V.tensor_copy(v_sb[:, s, :, 0:8], ps[:, 6, 256:512].rearrange("p (h d) -> p h d", d=XD)
                              ).then_inc(sem("kv_taken"), 1)

            def mean_squares(t, s):
                dve.wait_ge(sem("k_squared"), t + 1)
                V.tensor_reduce(kms[:, s % 2], ksq[:, s % 2].rearrange("p (h d) -> p h d", d=XD), AX_X, ALU.add
                                ).then_inc(sem("k_meansq"), 1)

            def pack_keys(t, s):
                dve.wait_ge(sem("k_rstd"), t + 1)
                knb = kn.rearrange("p (h d) -> p h d", d=XD)
                V.tensor_tensor(knb, kraw[:, s % 2].rearrange("p (h d) -> p h d", d=XD),
                                krs[:, s % 2, :, None].to_broadcast([P, XH, XD]), ALU.mult
                                ).then_inc(sem("k_normed"), 1)
                if not (isinstance(t, int) and t < 2):
                    dve.wait_ge(sem("k_transposed"), t - 1)
                dve.wait_ge(sem("k_normed"), t + 1)
                pack = kpack[:, s % 2].rearrange("p (h s r d) -> p h s r d", s=2, r=2, d=XD)
                kn2 = knb[:, :, None, :].to_broadcast([P, XH, 2, XD])
                V.tensor_copy(pack[:, :, :, 0], kn2).then_inc(sem("k_high"), 1)
                dve.wait_ge(sem("k_high"), t + 1)
                V.tensor_tensor(pack[:, :, :, 1], kn2, pack[:, :, :, 0], ALU.subtract
                                ).then_inc(sem("k_packed"), 1)

            def take_keys(t, s):
                dve.wait_ge(sem("k_transposed"), t + 1)
                if not (isinstance(t, int) and t < 2):
                    dve.wait_ge(sem("scores_done"), 4 * t - 4)
                V.tensor_copy(kT[:, s % 2], ps[:, 7].bitcast(F16).rearrange("p (g m) -> p g m", g=GROUPS)
                              ).then_inc(sem("k_ready"), 1)

            def kv_step(t, s):
                if not (isinstance(t, int) and t >= NB):
                    take_kv(t, s)
                if not (isinstance(t, int) and t < 2):
                    take_keys(t - 2, (s - 2) % 4)
                if not (isinstance(t, int) and not 1 <= t <= NB):
                    pack_keys(t - 1, (s - 1) % 4)
                if not (isinstance(t, int) and t >= NB):
                    mean_squares(t, s)

            def take_acc(b, c):
                V.tensor_copy(accs[:, b, c * 512:c * 512 + 512], ps[:, 4 + c]).then_inc(sem("acc_taken"), 1)

            copy_q(0)
            take_kv(0, 0)
            mean_squares_q(0)
            mean_squares(0, 0)
            pack_q(0)
            take_kv(1, 1)
            pack_keys(0, 0)
            take_q(0, 3)
            mean_squares(1, 1)
            copy_q(1)
            kv_step(2, 2)
            mean_squares_q(1)
            pack_q(1)
            kv_step(3, 3)
            take_q(1, 7)
            with dve.Fori(1, MB // 4) as q:
                for s in range(4):
                    kv_step(4 * q + s, s)
            for s in range(4):
                if s == 3:
                    dve.wait_ge(sem("pv_done"), ROUNDS * MB)
                    for c in range(2):
                        take_acc(0, c)
                kv_step(MB + s, s)
                if s < 3:
                    if s == 0:
                        dve.wait_ge(sem("w_ffn"), loaded["w_ffn"])
                    V.tensor_reduce(fsc[:, s:s + 1], w_ffn[:, s], AX_X, ALU.add, apply_absolute_value=True
                                    ).then_inc(sem("ffn_abs"), 1)
            dve.wait_ge(sem("ffn_summed"), 1)
            V.tensor_scalar(fsc[:, 3:6], ps[:, 7, 0:3], 1.0 / (HID * D), None, ALU.mult).then_inc(sem("ffn_scaled"), 1)
            dve.wait_ge(sem("ffn_scaled"), 1)
            step(dve, V.tensor_scalar(fsc[:, 6:9], fsc[:, 3:6], 0.5, None, ALU.mult))
            V.tensor_scalar(fsc[:, 9:12], fsc[:, 3:6], -0.5, None, ALU.mult).then_inc(sem("ffn_quarters"), 1)

            def ternary(q, s):
                w, n = q - (MB // 4 + 1), 4 * q + (s - MB - 3)
                src = w_flat[:, bass.ds(w * (4 * FCHUNK) + s * FCHUNK, FCHUNK)]
                dve.wait_ge(sem("ffn_quarters"), n)
                V.tensor_scalar(tern, src, fsc[:, bass.ds(w + 9, 1)], None, ALU.is_lt).then_inc(sem("ffn_below"), 1)
                dve.wait_ge(sem("ffn_below"), n)
                V.scalar_tensor_tensor(tern, src, fsc[:, bass.ds(w + 6, 1)], tern, ALU.is_gt, ALU.subtract
                                       ).then_inc(sem("ffn_above"), 1)
                dve.wait_ge(sem("ffn_above"), n)
                V.tensor_copy(t_flat[:, bass.ds(w * (4 * FCHUNK) + s * FCHUNK, FCHUNK)], tern
                              ).then_inc(sem("ffn_quarters"), 1)

            w_flat = w_ffn.rearrange("p w n -> p (w n)")
            t_flat = w_tern.rearrange("p w n -> p (w n)")
            with dve.Fori(MB // 4 + 1, NB // 4) as q:
                for s in range(4):
                    kv_step(4 * q + s, s)
                    ternary(q, s)
            kv_step(NB, 0)
            kv_step(NB + 1, 1)
            def add_context(b):
                if b == 0:
                    dve.wait_ge(sem("pv_done"), ROUNDS * NB - 2)
                    take_acc(1, 0)
                else:
                    dve.wait_ge(sem("pv_done"), ROUNDS * NB)
                    take_acc(1, 1)
                dve.wait_ge(sem("acc_transposed"), 2 * (b + 1))
                t = ps[:, 2 * b:2 * b + 2].rearrange("p c (h r) -> p (c h) r", r=32)
                step(dve, V.reciprocal(rden[:, b, :, None], t[:, :, 8:9]))
                step(dve, V.tensor_tensor(xn[:, b].rearrange("p (h d) -> p h d", d=XD), t[:, :, 0:8],
                                          rden[:, b, :, None].to_broadcast([P, XH, XD]), ALU.mult))
                step(dve, V.tensor_tensor(x[:, b], x[:, b], xn[:, b], ALU.add))
            vector_rest(dve, add_context)

        @block.gpsimd
        def _(pool):
            G = nc.gpsimd
            G.memset(uacc, 0.0).then_inc(sem("uacc_zero"), 1)
            G.memset(qbd, 0.0).then_inc(sem("qbd_zero"), 1)
            pool.wait_ge(sem("uacc_zero"), 1)

            def square_keys(t, s):
                pool.wait_ge(sem("k_taken"), t + 1)
                G.tensor_tensor(ksq[:, s % 2], kraw[:, s % 2], kraw[:, s % 2], ALU.mult).then_inc(sem("k_squared"), 1)

            def split_low(t, s):
                pool.wait_ge(sem("ctx_high"), t + 1)
                G.tensor_tensor(ctx_half[:, s % 2, 1], ctxT[:, s], ctx_half[:, s % 2, 0].bitcast(F32), ALU.subtract
                                ).then_inc(sem("ctx_split"), 1)

            def weigh_context(t, s, b, q4):
                pool.wait_ge(sem(f"ctx_loaded{s}"), 16 * (q4 + 1))
                if isinstance(t, int):
                    pool.wait_ge(sem("geo_ready"), 1)
                g = geo[:, None, bass.ds((t - MB * b) * P, P)].to_broadcast([P, KT, P])
                G.tensor_tensor(gprod[:, s % 2], ctxT[:, s], g, ALU.mult).then_inc(sem("ctx_weighed"), 1)
                pool.wait_ge(sem("ctx_weighed"), t + 1)
                G.tensor_tensor(uacc[:, b], uacc[:, b], gprod[:, s % 2], ALU.add).then_inc(sem("ctx_weighted"), 1)

            split_low(0, 0)
            pool.wait_ge(sem("wkv_high"), 1)
            G.tensor_tensor(wkv_half[:, 1], w_xkv, wkv_half[:, 0].bitcast(F32), ALU.subtract).then_inc(sem("wkv_split"), 1)
            split_low(1, 1)
            weigh_context(0, 0, 0, 0)
            square_keys(0, 0)
            split_low(2, 2)
            weigh_context(1, 1, 0, 0)
            square_keys(1, 1)
            split_low(3, 3)
            for t in range(2, 4):
                weigh_context(t, t, 0, 0)
            for b in range(B):
                with pool.Fori(b * (MB // 4 - 1), (b + 1) * MB // 4 - 1) as q:
                    for s in range(4):
                        square_keys(4 * q + (s + 2), s)
                        split_low(4 * q + (s + 4), s)
                        weigh_context(4 * q + (s + 4), s, b, q + 1)
            for t in range(NB - 2, NB):
                square_keys(t, t)
            pool_rest(pool)

        @block.scalar
        def _(act):
            nc.scalar.preload_act_table_set("natural_log_exp_and_others")
            ln_rstd(act, LN_OF["xattn"])
            act.wait_ge(sem("decay_loaded"), 16)
            nc.scalar.activation(dec[:, 0:1], decay[:], ACT.Exp, scale=-1.0).then_inc(sem("decay_exp"), 1)
            def square_q(b):
                act.wait_ge(sem("q_copied"), b + 1)
                nc.scalar.activation(qsq[:, b], qraw[:, b], ACT.Square).then_inc(sem("q_squared"), 1)

            def q_rstd(b):
                act.wait_ge(sem("q_meansq"), b + 1)
                nc.scalar.activation(qrs[:, b], qms[:, b], ACT.Ln, bias=1e-6, scale=1.0 / XD).then_inc(sem("q_log"), 1)
                act.wait_ge(sem("q_log"), b + 1)
                nc.scalar.activation(qrs[:, b], qrs[:, b], ACT.Exp, scale=-0.5).then_inc(sem("q_rstd"), 1)

            def split_high(t, s, q4):
                act.wait_ge(sem(f"ctx_loaded{s}"), 16 * (q4 + 1))
                if not (isinstance(t, int) and t < 2):
                    act.wait_ge(sem("kv_projected"), t - 1)
                nc.scalar.copy(ctx_half[:, s % 2, 0], ctxT[:, s]).then_inc(sem("ctx_high"), 1)

            split_high(0, 0, 0)
            act.wait_ge(sem("wkv_loaded"), 16)
            nc.scalar.copy(wkv_half[:, 0], w_xkv).then_inc(sem("wkv_high"), 1)
            split_high(1, 1, 0)
            square_q(0)
            q_rstd(0)

            def key_rstd(t, s):
                act.wait_ge(sem("k_meansq"), t + 1)
                nc.scalar.activation(kln, kms[:, s % 2], ACT.Ln, bias=1e-6, scale=1.0 / XD).then_inc(sem("k_log"), 1)
                act.wait_ge(sem("k_log"), t + 1)
                nc.scalar.activation(krs[:, s % 2], kln, ACT.Exp, scale=-0.5).then_inc(sem("k_rstd"), 1)

            def exps(t, s, r):
                act.wait_ge(sem("scores_done"), 4 * t + r + 1)
                if not (isinstance(t, int) and t < 1):
                    act.wait_ge(sem("pv_done"), 4 * t + r - 3)
                nc.scalar.activation(probs[:, r].rearrange("p a g j n -> p a (g j n)"), ps[:, 2 * (r % 2):2 * (r % 2) + 2],
                                     ACT.Exp, scale=XD ** -0.5).then_inc(sem("exp_done"), 1)

            for t in range(2):
                key_rstd(t, t)
                split_high(t + 2, t + 2, 0)

            def act_step(t, s, q4):
                for r in range(ROUNDS):
                    exps(t, s, r)
                    if r == 0 and not (isinstance(t, int) and t + 2 >= NB):
                        key_rstd(t + 2, (s + 2) % 4)
                    if isinstance(t, int) and t == 0 and r < 2:
                        (square_q, q_rstd)[r](1)
                    if r == 0 and not (isinstance(t, int) and t + 4 >= NB):
                        split_high(t + 4, s, q4 + 1)

            for t in range(4):
                act_step(t, t, 0)
                share = -(-len(loads) // 4)
                for name, dst, src in loads[share * t:share * (t + 1)]:
                    act.dma_start(dst, src).then_inc(sem(name), 16)
            with act.Fori(1, NB // 4 - 1) as q:
                for s in range(4):
                    act_step(4 * q + s, s, q)
            for t in range(NB - 4, NB):
                act_step(t, t % 4, NB // 4 - 1)
            scalar_rest(act)

        @block.tensor
        def _(pe):
            T = nc.tensor
            def project(t, s):
                pe.wait_ge(sem("ctx_split"), t + 1)
                if not (isinstance(t, int) and t < 1):
                    pe.wait_ge(sem("kv_taken"), t)
                for n, (c, d) in enumerate(HALF_PRODUCTS):
                    if isinstance(t, int) and t == 0 and n != 1:
                        pe.wait_ge(sem(("wkv_high", None, "wkv_split")[n]), 1)
                    for kt in range(KT):
                        i = T.matmul(ps[:, 6], ctx_half[:, s % 2, c, kt], wkv_half[:, d, kt], start=(n + kt == 0),
                                     stop=(n == 2 and kt == KT - 1))
                i.then_inc(sem("kv_projected"), 1)

            pe.wait_ge(sem("ones_set"), 1)
            keep_warm(WARM[LN_OF["xattn"]], 0)
            pe.wait_ge(sem("x_loaded"), 32)
            ln_transpose(pe, LN_OF["xattn"], 0)
            pe.wait_ge(sem("xnT_ready"), 1)
            pe.wait_ge(sem("wq_loaded"), 16)
            for b in range(B):
                for kt in range(KT):
                    i = T.matmul(ps[:, 1 + b, 0:256], xnT[:, kt, b, 3:], w_xq[:, kt], start=(kt == 0), stop=(kt == KT - 1))
                i.then_inc(sem("q_projected"), 1)
                if b == 0:
                    project(0, 0)
            pe.wait_ge(sem("zeros_set"), 1)

            def turn_keys(t, s):
                pe.wait_ge(sem("k_packed"), t + 1)
                if isinstance(t, int) and t == MB + 2:
                    pe.wait_ge(sem("ffn_scaled"), 1)
                if isinstance(t, int) and t == 2:
                    pe.wait_ge(sem("q_ready"), 2)
                if not (isinstance(t, int) and t < 1):
                    pe.wait_ge(sem("k_ready"), t)
                out = ps[:, 7].bitcast(F16)
                for g in range(GROUPS):
                    i = T.transpose(out[:, g * P:(g + 1) * P], kpack[:, s % 2, g * P:(g + 1) * P], id16[:])
                i.then_inc(sem("k_transposed"), 1)

            def scores(b, t, s, r):
                if not (isinstance(t, int) and 4 * t + r < 2):
                    pe.wait_ge(sem("exp_done"), 4 * t + r - 1)
                for gg in range(2):
                    g = 2 * r + gg
                    for a in range(2):
                        rows = slice(64 * a, 64 * a + 64)
                        i = T.matmul(ps[:, 2 * (r % 2) + a, gg * 256:gg * 256 + 256], kT[rows, s % 2, g],
                                     qbd[rows, b, g], start=True, stop=True)
                i.then_inc(sem("scores_done"), 1)

            def values(s, r):
                for gg in range(2):
                    g = 2 * r + gg
                    for j in range(4):
                        i = T.matmul(ps[32 * j:32 * j + 9, 4 + g // 4, (g % 4) * P:(g % 4 + 1) * P],
                                     v_sb[:, s, 4 * g + j], probs[:, r, j // 2, gg, j % 2],
                                     start=False, stop=False, skip_group_check=True)
                i.then_inc(sem("pv_done"), 1)

            def open_acc():
                for c in range(2):
                    T.matmul(ps[:, 4 + c], zer[:, 0:128], zer, start=True, stop=False, skip_group_check=True)

            def pe_step(b, t, s, q4):
                tt = t if isinstance(t, int) else None
                for r in range(ROUNDS):
                    if r == 0:
                        pe.wait_ge(sem("k_ready"), t + 1)
                    scores(b, t, s, r)
                    if tt == 0 and r < 2:
                        pass
                    else:
                        if tt == MB and r == 2:
                            pe.wait_ge(sem("acc_taken"), 2)
                            open_acc()
                        if r < 2:
                            values((s - 1) % 4, r + 2)
                        else:
                            values(s, r - 2)
                    if r == 0 and not (tt is not None and tt + 3 >= NB):
                        s3 = (s + 3) % 4
                        project(t + 3, s3)
                    if r == 1 and not (tt is not None and tt + 1 >= NB):
                        turn_keys(t + 1, (s + 1) % 4)

            def turn_queries(b, bank):
                pe.wait_ge(sem("q_packed"), b + 1)
                for g in range(GROUPS):
                    i = T.transpose(ps[:, bank].bitcast(F16)[:, g * P:(g + 1) * P], qpack[:, b, g * P:(g + 1) * P], id16[:])
                i.then_inc(sem("q_transposed"), 1)

            open_acc()
            project(1, 1)
            pe.wait_ge(sem("id16_loaded"), 16)
            turn_queries(0, 3)
            turn_keys(0, 0)
            project(2, 2)
            pe.wait_ge(sem("q_ready"), 1)
            pe.wait_ge(sem("q_copied"), 2)
            for t in range(4):
                pe_step(0, t, t, 0)
                if t == 0:
                    pe.wait_ge(sem("k_ready"), 2)
                    turn_queries(1, 7)
            with pe.Fori(1, MB // 4) as q:
                for s in range(4):
                    pe_step(0, 4 * q + s, s, q)
            for s in range(4):
                pe_step(1, MB + s, s, MB // 4)
                if s == 0:
                    pe.wait_ge(sem("k_ready"), MB + 2)
                    pe.wait_ge(sem("ffn_abs"), 3)
                    pe.wait_ge(sem("ones_set"), 1)
                    T.matmul(ps[:, 7, 0:3], ones[:], fsc[:, 0:3], start=True, stop=True).then_inc(sem("ffn_summed"), 1)
            with pe.Fori(MB // 4 + 1, NB // 4 - 1) as q:
                for s in range(4):
                    pe_step(1, 4 * q + s, s, q)
            for s in range(4):
                pe_step(1, NB - 4 + s, s, NB // 4 - 1)
            def turn_acc(b, c):
                pe.wait_ge(sem("acc_taken"), 2 * b + c + 1)
                for g in range(4 * c, 4 * c + 4):
                    i = T.transpose(ps[:, 2 * b + c, (g % 4) * P:(g % 4 + 1) * P], accs[:, b, g * P:(g + 1) * P], id32[:])
                i.then_inc(sem("acc_transposed"), 1)

            pe.wait_ge(sem("exp_done"), ROUNDS * NB - 1)
            values(3, 2)
            for c in range(2):
                turn_acc(0, c)
            pe.wait_ge(sem("exp_done"), ROUNDS * NB)
            values(3, 3)
            for c in range(2):
                turn_acc(1, c)
            tensor_rest(pe)


def layout(inputs):
    import numpy as np

    f = {k: np.asarray(v) for k, v in inputs.items()}
    A = {}

    def tiles(a):
        return a.reshape(-1, P, a.shape[-1]).transpose(1, 0, 2)

    def rows(a):
        return np.broadcast_to(a.reshape(1, -1), (P, a.size))

    def padded(a, n):
        return np.concatenate([a, np.zeros((n - a.shape[0],) + a.shape[1:], a.dtype)])

    A["x"] = f["x"]
    c = f["ctx_2048"][:, ::-1].reshape(B, MB, P, KT, P)
    A["ctx"] = c.transpose(0, 1, 4, 3, 2).reshape(NB, P, KT, P)
    A["w_xq"] = tiles(f["L0_xattn_Wq"].T)
    kv = np.concatenate([f["L0_xattn_Wk"], f["L0_xattn_Wv"]])
    A["w_xkv"] = tiles(np.concatenate([kv[0::2], kv[1::2]]).T)
    for n in "qkv":
        A[f"w_{n}"] = tiles(f[f"L0_attn_w_{n}"])
    A["w_o"] = tiles(f["L0_attn_w_o"])
    A["b_qkv"] = np.stack([f[f"L0_attn_b_{n}"].reshape(AH, AD).T for n in "qkv"], 1)
    A["b_o"] = rows(f["L0_attn_b_o"])
    w1, w3 = (tiles(padded(f[f"L0_ffn_{n}"], HT_FFN * P).T).reshape(P, -1) for n in ("w1", "w3"))
    w2 = tiles(padded(f["L0_ffn_w2"].T, HT_FFN * P)).reshape(P, -1)
    A["w_ffn"] = np.stack([w1, w3, w2], 1)
    A["decay"] = rows(f["L1_xattn_decay"].reshape(1))
    A["w_in"] = tiles(f["L1_xattn_W_in"].T)
    A["w_out1"] = tiles(f["L1_xattn_W_out"].T)
    A["b_in"] = f["L1_xattn_b_in"].reshape(KT, P).T
    A["vecs"] = np.stack([rows(f[f"L1_xattn_{n}"]) for n in ("b_out", "gamma", "beta")], 1)
    A["w_mem"] = tiles(f["L1_attn_W_mem"])
    A["w_conv"] = np.broadcast_to(f["L1_attn_conv_k"].reshape(1, CONV, 288), (P, CONV, 288))
    q = f["L1_attn_W_q"].reshape(D, 4, CH * CM, 2).transpose(0, 1, 3, 2)
    A["w_q4"] = tiles(np.concatenate([q, q], 3).reshape(D, 1024))
    A["theta"] = rows(f["L1_attn_theta"])
    w = np.zeros((2, FT, 2, CH, CM, 2, SW), np.float32)
    for c, n in enumerate(("W_re", "W_im")):
        a = f[f"L1_attn_{n}"].reshape(FT, 2, CH, 1, SW)
        for k in range(2):
            w[c, :, k, :, :, k] = a[:, k]
    A["w_ri"] = w.reshape(2, FT, P, 96).transpose(2, 0, 1, 3)
    A["w_nrm"] = np.broadcast_to(f["L1_attn_norm_scale"].reshape(FT, 2 * CH, 1), (FT, 2 * CH, CM)).reshape(FT, P).T
    l = np.arange(P, dtype=np.float32)[:, None]
    dist = np.concatenate([np.broadcast_to(l - (L - 1), (P, 28)), np.broadcast_to(-l, (P, 4))], 1)
    slopes = np.concatenate([f["L1_attn_decay_slopes"], f["L1_attn_anchor_slopes"]])
    A["small"] = np.stack([rows(slopes), rows(f["L1_attn_score_scale"]), dist], 1)
    A["w_out2"] = tiles(f["L1_attn_W_out"])
    A["w_rt"] = tiles(np.concatenate([f["L1_ffn_gate_w"], f["L1_ffn_shared_gate_vec"]]).T)
    shared = f["L1_ffn_shared_gate_up"].reshape(2, 4, EI, D).transpose(1, 0, 2, 3).reshape(4, 2 * EI, D)
    gu = np.concatenate([f["L1_ffn_expert_gate_up"], shared]).reshape(UNITS * 2 * EI, D)
    A["w_gu"] = gu.T.reshape(KT, P, UNITS * 2 * EI)
    down = np.concatenate([f["L1_ffn_expert_down"].transpose(0, 2, 1).reshape(E * EI, D), f["L1_ffn_shared_down"].T])
    A["w_down"] = tiles(padded(down, DT * P))
    A["id32"] = np.eye(P, dtype=np.float32)
    A["id16"] = np.eye(P, dtype=np.float16)
    A["tri"] = np.triu(np.ones((P, P), np.float32))
    A["mask"] = np.where(np.tril(np.ones((P, P))) > 0, 0.0, -1e10).astype(np.float32)
    A["iota"] = rows(np.arange(E, dtype=np.float32))
    return {k: np.ascontiguousarray(v) for k, v in A.items()}


def kernel(**inputs):
    import concourse.bacc as bacc
    from concourse.bass_utils import run_bass_kernel_spmd

    nc = bacc.Bacc("TRN2", target_bir_lowering=False, num_devices=1)
    io, arrays = {}, {}
    for name, a in layout(inputs).items():
        arrays[f"in_{name}"] = a
        io[name] = nc.dram_tensor(f"in_{name}", a.shape, mybir.dt.from_np(a.dtype), kind="ExternalInput").ap()
    io["out"] = nc.dram_tensor("out", (B, L, D), F32, kind="ExternalOutput").ap()
    build_program(nc, io)
    return run_bass_kernel_spmd(nc, [arrays], core_ids=[0]).results[0]["out"]
```
